# Optimizing a Trainium2 kernel written in Bass

```python
import numpy as np
import jax
import jax.numpy as jnp

def _softmax(x, axis=-1):
    return jax.nn.softmax(x, axis=axis)

def _gelu(x):
    return jax.nn.gelu(x, approximate=True)

def _silu(x):
    return jax.nn.silu(x)

def _sigmoid(x):
    return jax.nn.sigmoid(x)

def _layernorm(x, axis=-1, eps=1e-05):
    m = jnp.mean(x, axis=axis, keepdims=True)
    v = jnp.var(x, axis=axis, keepdims=True)
    return (x - m) / jnp.sqrt(v + eps)

def _scatter_add(tgt, idx, src, axis=0):
    return tgt.at[idx].add(src)

def _segment_sum(src, seg, n):
    return jax.ops.segment_sum(src, seg, n)
kernel_name = 'mk_xattn_ffn_d1_seqx_r4_a34fef'

def setup_inputs(seed: int=0):
    np.random.seed(seed)
    _w = jnp.asarray

    def _rec_inputs():
        import jax
        import jax.numpy as jnp
        _rk = jax.random.key(seed)
        x = -0.0002928 + 1 * jax.random.normal(jax.random.fold_in(_rk, 1), (16, 112, 256), jnp.float32)
        _lenS = 112 - jax.random.randint(jax.random.fold_in(_rk, 7), (16,), 0, max(1, 112 // 4) + 1, jnp.int32)
        _lenS2 = 375 - jax.random.randint(jax.random.fold_in(_rk, 8), (16,), 0, max(1, 375 // 4) + 1, jnp.int32)
        _ctx_1024P = jax.random.normal(jax.random.fold_in(_rk, 11), (16, 16, 256), jnp.float32)
        _ctx_1024c = jax.random.dirichlet(jax.random.fold_in(_rk, 511), 0.3 * jnp.ones((16,), jnp.float32), (16, 375))
        _ctx_1024t = jnp.einsum('bsk,bkd->bsd', _ctx_1024c, _ctx_1024P)
        _ctx_1024t = _ctx_1024t * jax.lax.rsqrt(jnp.mean(jnp.square(_ctx_1024t)) + 1e-12) * 0.953939
        ctx_1024 = -1.39393e-06 + 0.999914 * (_ctx_1024t + 0.3 * jax.random.normal(jax.random.fold_in(_rk, 611), (16, 375, 256), jnp.float32))
        return (x, ctx_1024)
    x, ctx_1024 = _rec_inputs()

    def _L0_xattn_setup():
        import jax, jax.numpy as jnp
        import numpy as np
        EMBED_DIM = 256
        NUM_HEADS = 16
        HEAD_DIM = EMBED_DIM // NUM_HEADS
        SCALE = HEAD_DIM ** (-0.5)
        key = jax.random.key(seed)
        ks = jax.random.split(key, 8)
        B, Nq, Nkv, C = (2, 512, 512, EMBED_DIM)
        s = C ** (-0.5)
        return {'q': jax.random.normal(ks[0], (B, Nq, C), dtype=jnp.float32), 'kv': jax.random.normal(ks[1], (B, Nkv, C), dtype=jnp.float32), 'w_q': jax.random.normal(ks[2], (C, C), dtype=jnp.float32) * s, 'b_q': jnp.zeros((C,), dtype=jnp.float32), 'w_kv': jax.random.normal(ks[3], (C, 2 * C), dtype=jnp.float32) * s, 'b_kv': jnp.zeros((2 * C,), dtype=jnp.float32), 'w_out': jax.random.normal(ks[4], (C, C), dtype=jnp.float32) * s, 'b_out': jnp.zeros((C,), dtype=jnp.float32)}
    _L0_xattn_all = _L0_xattn_setup()
    _L0_xattn_in = {k: v for k, v in _L0_xattn_all.items() if k in ('w_q', 'b_q', 'w_kv', 'b_kv', 'w_out', 'b_out')}
    del _L0_xattn_all

    def _L0_ffn_setup():
        import jax, jax.numpy as jnp
        import numpy as np
        H = 256
        DFF = 1024
        E = 8
        B = 8
        S = 128
        INIT_LAMBDA = 0.2
        key = jax.random.key(seed)
        ks = jax.random.split(key, 9)
        hidden_states = jax.random.normal(ks[0], (S, B, H), dtype=jnp.float32)
        gW1 = 0.01 * jax.random.normal(ks[1], (H, H), dtype=jnp.float32)
        gb1 = jnp.zeros((H,), dtype=jnp.float32)
        gW2 = 0.01 * jax.random.normal(ks[2], (E, H), dtype=jnp.float32)
        gb2 = jnp.full((E,), INIT_LAMBDA, dtype=jnp.float32)
        sc1 = 1.0 / np.sqrt(H)
        sc2 = 1.0 / np.sqrt(DFF)
        eW1 = sc1 * jax.random.normal(ks[3], (E, DFF, H), dtype=jnp.float32)
        eb1 = sc1 * jax.random.normal(ks[4], (E, DFF), dtype=jnp.float32)
        eW2 = sc2 * jax.random.normal(ks[5], (E, H, DFF), dtype=jnp.float32)
        eb2 = sc2 * jax.random.normal(ks[6], (E, H), dtype=jnp.float32)
        return {'hidden_states': hidden_states, 'gW1': gW1, 'gb1': gb1, 'gW2': gW2, 'gb2': gb2, 'eW1': eW1, 'eb1': eb1, 'eW2': eW2, 'eb2': eb2}
    _L0_ffn_all = _L0_ffn_setup()
    _L0_ffn_in = {k: v for k, v in _L0_ffn_all.items() if k in ('gW1', 'gb1', 'gW2', 'gb2', 'eW1', 'eb1', 'eW2', 'eb2')}
    del _L0_ffn_all
    return {'x': x, 'ctx_1024': ctx_1024, 'L0_xattn_w_q': _L0_xattn_in['w_q'], 'L0_xattn_b_q': _L0_xattn_in['b_q'], 'L0_xattn_w_kv': _L0_xattn_in['w_kv'], 'L0_xattn_b_kv': _L0_xattn_in['b_kv'], 'L0_xattn_w_out': _L0_xattn_in['w_out'], 'L0_xattn_b_out': _L0_xattn_in['b_out'], 'L0_ffn_gW1': _L0_ffn_in['gW1'], 'L0_ffn_gb1': _L0_ffn_in['gb1'], 'L0_ffn_gW2': _L0_ffn_in['gW2'], 'L0_ffn_gb2': _L0_ffn_in['gb2'], 'L0_ffn_eW1': _L0_ffn_in['eW1'], 'L0_ffn_eb1': _L0_ffn_in['eb1'], 'L0_ffn_eW2': _L0_ffn_in['eW2'], 'L0_ffn_eb2': _L0_ffn_in['eb2']}

def reference(x, ctx_1024, L0_xattn_w_q, L0_xattn_b_q, L0_xattn_w_kv, L0_xattn_b_kv, L0_xattn_w_out, L0_xattn_b_out, L0_ffn_gW1, L0_ffn_gb1, L0_ffn_gW2, L0_ffn_gb2, L0_ffn_eW1, L0_ffn_eb1, L0_ffn_eW2, L0_ffn_eb2):
    import jax
    import jax.numpy as jnp

    def _L0_xattn_ref(q, kv, w_q, b_q, w_kv, b_kv, w_out, b_out):
        import jax, jax.numpy as jnp
        import numpy as np
        EMBED_DIM = 256
        NUM_HEADS = 16
        HEAD_DIM = EMBED_DIM // NUM_HEADS
        SCALE = HEAD_DIM ** (-0.5)
        B, Nq, C = q.shape
        _, Nkv, _ = kv.shape
        H, D = (NUM_HEADS, HEAD_DIM)
        qp = (q @ w_q + b_q).reshape(B, Nq, H, D).transpose(0, 2, 1, 3)
        kvp = (kv @ w_kv + b_kv).reshape(B, Nkv, 2, H, D).transpose(2, 0, 3, 1, 4)
        kp, vp = (kvp[0], kvp[1])
        attn = jnp.einsum('bhqd,bhkd->bhqk', qp, kp) * SCALE
        attn = jax.nn.softmax(attn, axis=-1)
        out = jnp.einsum('bhqk,bhkd->bhqd', attn, vp)
        out = out.transpose(0, 2, 1, 3).reshape(B, Nq, C)
        return out @ w_out + b_out

    def _L0_ffn_ref(hidden_states, gW1, gb1, gW2, gb2, eW1, eb1, eW2, eb2):
        import jax, jax.numpy as jnp
        import numpy as np
        H = 256
        DFF = 1024
        E = 8
        B = 8
        S = 128
        INIT_LAMBDA = 0.2
        x = jnp.transpose(hidden_states, (1, 0, 2))
        h = jax.nn.relu(jnp.einsum('bsh,oh->bso', x, gW1) + gb1)
        gate = jnp.einsum('bsh,eh->bse', h, gW2) + gb2
        g = gate.mean(axis=1)
        W1 = jnp.einsum('be,eoi->boi', g, eW1)
        b1 = g @ eb1
        W2 = jnp.einsum('be,eoi->boi', g, eW2)
        b2 = g @ eb2
        y = jax.nn.relu(jnp.einsum('bsi,boi->bso', x, W1) + b1[:, None, :])
        y = jnp.einsum('bsi,boi->bso', y, W2) + b2[:, None, :]
        return jnp.transpose(y, (1, 0, 2))
    x = x + _L0_xattn_ref(_layernorm(x, axis=-1), ctx_1024, L0_xattn_w_q, L0_xattn_b_q, L0_xattn_w_kv, L0_xattn_b_kv, L0_xattn_w_out, L0_xattn_b_out)
    x = x + _L0_ffn_ref(_layernorm(x, axis=-1), L0_ffn_gW1, L0_ffn_gb1, L0_ffn_gW2, L0_ffn_gb2, L0_ffn_eW1, L0_ffn_eb1, L0_ffn_eW2, L0_ffn_eb2)
    return x

_drawn_inputs = setup_inputs


def setup_inputs(seed=0):
    import zlib

    import numpy as np

    out = dict(_drawn_inputs(seed))
    spreads = {'L0_xattn_b_q': (0.0, 0.417),
     'L0_xattn_b_kv': (0.0, 0.1),
     'L0_xattn_b_out': (0.0, 0.1),
     'L0_ffn_gb1': (0.0, 0.661),
     'L0_ffn_gb2': (0.20000000298023224, 0.2)}
    factors = {'L0_ffn_gW1': 8.0, 'L0_ffn_eb1': 4.924, 'L0_ffn_eb2': 3.748}
    for name, (base, spread) in spreads.items():
        noise = np.random.default_rng([zlib.crc32(name.encode()), seed]).standard_normal(out[name].shape)
        drawn = base * np.exp(spread * noise) if base else spread * noise
        out[name] = jnp.asarray(drawn.astype(out[name].dtype))
    for name, factor in factors.items():
        out[name] = (out[name] * factor).astype(out[name].dtype)
    return out
```

```python
from contextlib import ExitStack

import concourse.bass as bass
from concourse import mybir

F32 = mybir.dt.float32
F32R = mybir.dt.float32r
BF16 = mybir.dt.bfloat16
I32 = mybir.dt.int32
ALU = mybir.AluOpType
ACT = mybir.ActivationFunctionType
AX_X = mybir.AxisListType.X

P = 128
B, NQ, C = 16, 112, 256
NKV = 375
KVE = NKV + 1
KVP = 384
CH = KVP // P
CHROWS = [P, P, NKV - 2 * P]
H, D = 16, 16
HH = H // 2
SCALE = float(D) ** -0.5
EPS = 1e-5
MAGIC = 0x5EF759DF
ROOT_STEPS = 3
ROOT_OPS = 1 + 4 * ROOT_STEPS
T = B * NQ
TT = T // P
PAT = NQ // 16
DFF, E = 1024, 8
IT = C // P
OT = DFF // P
GB = 4
NG = B // GB
GW = GB * NQ
VW = 2 * D
GCOLS = DFF + C + E
QROWS = 6 * D
SROWS = QROWS + 2


class Batch:

    def __init__(self, c, i=None):
        self.c, self.i = c, i

    def __add__(self, n):
        return Batch(self.c + n, self.i)

    @property
    def exists(self):
        return self.i is not None or 0 <= self.c < B

    @property
    def slot(self):
        return self.c % 2

    def times(self, per, more=0, of=B):
        if self.i is None:
            return min(per * self.c + more, per * of)
        return self.i * (2 * per) + (per * self.c + more)

    def uses(self, per):
        if self.i is None:
            return per * (self.c // 2 + 1)
        return self.i * per + per * (self.c // 2 + 1)


FIRST_STEP, LOOP_STEP, LOOPS, LAST_STEP = -3, 2, 5, 17


def steps(eng, step):
    for s in range(FIRST_STEP, LOOP_STEP):
        step(Batch(s))
    with eng.Fori(0, LOOPS) as i:
        for s in range(LOOP_STEP, LOOP_STEP + 2):
            step(Batch(s, i))
    for s in range(LOOP_STEP + 2 * LOOPS, LAST_STEP + 1):
        step(Batch(s))


def need(eng, sem, value):
    if isinstance(value, int) and value <= 0:
        return
    eng.wait_ge(sem, value)


def build(nc, x, ctx_t, wq, bq, wk, bk, wv, bv, wo, bo, gw1, gb1, gw2, gb2, w1, eb, w2, out):
    with ExitStack() as stack:
        def psum(name, shape, dt=F32):
            return stack.enter_context(nc.psum_tensor(name, shape, dt))

        def sem(name):
            return stack.enter_context(nc.semaphore(name))

        def size(shape, dt):
            n = 2 if dt == BF16 else 4
            for d in shape[1:]:
                n *= d
            return n

        class Region:

            def __init__(self, start, end):
                self.at, self.end = start, end

            def take(self, name, shape, dt):
                t = nc.alloc_sbuf_tensor_at(name, shape, dt, offset=self.at)
                self.at += (size(shape, dt) + 31) // 32 * 32
                assert self.at <= self.end, (name, self.at, self.end)
                return t

        start = (nc.sbuf_base + 31) // 32 * 32
        RAW = 2 * IT * 512 * 4
        W1B = 2 * 2 * IT * 512 * 4
        XTB = 2 * IT * T * 4
        W2B = 2 * 2 * OT * 512 * 4
        at_w2 = start + RAW
        at_w1 = at_w2 + W2B - XTB - W1B
        at_xt = at_w1 + W1B
        at_main = at_xt + XTB

        w_raw = nc.alloc_sbuf_tensor_at("w_raw", [P, 2, IT, 512], F32, offset=start)
        w1_parts = nc.alloc_sbuf_tensor_at("w1_parts", [P, 2, 2, IT, 512], F32R, offset=at_w1)
        xt_parts = nc.alloc_sbuf_tensor_at("xt_parts", [P, 2, IT, T], F32R, offset=at_xt)
        w2_parts = nc.alloc_sbuf_tensor_at("w2_parts", [P, 2, OT // 2, 2, 2, 512], F32R, offset=at_w2)

        ffn = Region(at_main, nc.sbuf_usable_end)
        gates = ffn.take("gates", [P, PAT, C + E], F32)
        y = ffn.take("y", [P, TT, C], F32)
        at_acc = ffn.at
        acc = ffn.take("acc", [P, TT, DFF], F32)
        h_high = nc.alloc_sbuf_tensor_at("h_high", [P, TT, OT, P], F32R, offset=at_acc)
        h_low = ffn.take("h_low", [P, TT, OT, P], F32R)
        keep = Region(ffn.at, nc.sbuf_usable_end)
        ident = keep.take("ident", [P, P], F32)
        ident_b = keep.take("ident_b", [P, P], BF16)
        ident_e = keep.take("ident_e", [E, E], F32)
        bq_sb = keep.take("bq_sb", [P, 2], F32)
        bk_sb = keep.take("bk_sb", [P, 2], F32)
        bv_sb = keep.take("bv_sb", [P, 2], F32)
        gb1_sb = keep.take("gb1_sb", [P, 2], F32)
        gb2_sb = keep.take("gb2_sb", [E, 1], F32)
        gw2_sb = keep.take("gw2_sb", [P, 2, E], F32)
        gate_t = keep.take("gate_t", [E, NQ], F32)
        max_rows = keep.take("max_rows", [D, 2, NQ], BF16)
        stats = keep.take("stats", [NQ, GB, 6], F32)
        mean_var = keep.take("mean_var", [NQ, GB, 2], F32)
        half_var = keep.take("half_var", [NQ, GB], F32)
        magic = keep.take("magic", [NQ, GB], I32)
        one_half = keep.take("one_half", [NQ, GB], F32)
        half_bits = keep.take("half_bits", [NQ, GB], I32)
        root_tmp = keep.take("root_tmp", [NQ, GB], F32)
        rstd = keep.take("rstd", [NQ, GB], F32)
        maxima = keep.take("maxima", [NQ, 2, H], F32)
        max_parts = keep.take("max_parts", [NQ, 2, 2, HH], BF16)
        recip = keep.take("recip", [NQ, H], F32)

        front = Region(at_w2, at_w1)
        k_f32 = front.take("k_f32", [P, 2, KVE], F32)
        k_rest = front.take("k_rest", [P, 2, KVE], F32)
        k_parts = front.take("k_parts", [P, 3, 2, KVP], BF16)
        o_full = front.take("o_full", [P, 4 * NQ], F32)
        o_norm = front.take("o_norm", [NQ, H, D], F32)
        ot_high = front.take("ot_high", [P, 2, NQ], F32R)
        ot_low = front.take("ot_low", [P, 2, NQ], F32R)
        x_norm = front.take("x_norm", [NQ, C], F32)
        x_bias = front.take("x_bias", [NQ, C], F32)
        x_mid = front.take("x_mid", [NQ, 2, C], F32)

        main = Region(at_main, ffn.at)
        w_f32 = main.take("w_f32", [P, 5, IT, C], F32)
        w_high = main.take("w_high", [P, 5, IT, C], F32R)
        w_low = main.take("w_low", [P, 5, IT, C], F32R)
        x_all = main.take("x_all", [NQ, B, C], F32)
        probs = main.take("probs", [P, 2 * CH, 2, 4 * NQ], F32)
        v_ones = main.take("v_ones", [P, 2, CH, H, VW], F32)
        q_stack = main.take("q_stack", [P, 2, H * NQ], BF16)
        at_ks = main.at
        k_stack = main.take("k_stack", [P, 2, H, KVP], BF16)
        pre = Region(at_ks, main.at)
        xq = pre.take("xq", [NQ, GB, C], F32)
        xqt_high = pre.take("xqt_high", [P, IT, GW], F32R)
        xqt_low = pre.take("xqt_low", [P, IT, GW], F32R)
        q_f32 = pre.take("q_f32", [P, GB, 2, NQ], F32)
        q_parts = pre.take("q_parts", [P, 3, GB, 2, NQ], BF16)
        at_ctx = main.at
        c_raw = main.take("c_raw", [P, 2, IT, KVE], F32)
        c_high = main.take("c_high", [P, 2, IT, KVE], F32R)
        c_low = main.take("c_low", [P, 2, IT, KVE], F32R)
        bias_row = main.take("bias_row", [NQ, C], F32)
        bo_row = main.take("bo_row", [NQ, C], F32)
        bv_wide = main.take("bv_wide", [P, 2, NQ], F32)
        gate = Region(at_ctx, main.at)
        g_relu = gate.take("g_relu", [P, 2, GW], F32)
        h_sums = gate.take("h_sums", [P, 2, NG, NQ], F32)
        h_sum = gate.take("h_sum", [P, 2, NQ], F32)
        eb_sb = gate.take("eb_sb", [E, GCOLS], F32)
        g_row = gate.take("g_row", [NQ, GCOLS], F32)
        q_rest = nc.alloc_sbuf_tensor_at("q_rest", [P, GB, 2, NQ], F32, offset=at_w1)

        WQ, WK, WV, WO, GW1 = range(5)

        k_dram = nc.dram_tensor("k_dram", [2, 3, D, H * KVP], BF16, kind="Internal").ap()
        q_dram = nc.dram_tensor("q_dram", [B, 3, D, H * NQ], BF16, kind="Internal").ap()
        xmid_dram = nc.dram_tensor("xmid_dram", [T, C], F32, kind="Internal").ap()
        gate_dram = nc.dram_tensor("gate_dram", [2 * NQ, GCOLS], F32, kind="Internal").ap()

        banks = psum("banks", [P, 8, 512])
        ps_max = banks[:, 0:2, :]
        ps_max_t = banks[0:D, 0, 384:448].bitcast(BF16)[:, 0:NQ]
        ps_sc = banks[:, 2:6, :]
        ps_o = banks[:, 6, :]
        ps_w = banks[:, 7, :]

        x_loaded = [sem(f"x_loaded{g}") for g in range(NG)]
        wq_loaded, w_loaded, small_loaded = sem("wq_loaded"), sem("w_loaded"), sem("small_loaded")
        ones_set, zero_set, ident_set = sem("ones_set"), sem("zero_set"), sem("ident_set")
        stack_set, pad_set = sem("stack_set"), sem("pad_set")
        w_high_done, w_low_done = sem("w_high_done"), sem("w_low_done")
        bv_wide_done, bias_mm, bias_done = sem("bv_wide_done"), sem("bias_mm"), sem("bias_done")
        q_stat, q_aggr, q_norm = sem("q_stat"), sem("q_aggr"), sem("q_norm")
        root_set, eps_added, bits_halved, root_done = sem("root_set"), sem("eps_added"), sem("bits_halved"), sem("root_done")
        q_tr, q_xhigh, q_xlow, q_mm = sem("q_tr"), sem("q_xhigh"), sem("q_xlow"), sem("q_mm")
        q_evac, q1_done, qr_done, q2_done, q3_done = (
            sem("q_evac"), sem("q1_done"), sem("qr_done"), sem("q2_done"), sem("q3_done"))
        q_stored = sem("q_stored")
        c_loaded = [sem("c_loaded0"), sem("c_loaded1")]
        c_high_done, c_low_done = sem("c_high_done"), sem("c_low_done")
        k_mm, v_mm, k_evac, v_evac = sem("k_mm"), sem("v_mm"), sem("k_evac"), sem("v_evac")
        k1_done, kr_done, k2_done, k3_done = sem("k1_done"), sem("kr_done"), sem("k2_done"), sem("k3_done")
        k_stored = sem("k_stored")
        stack_loaded = [[sem(f"stack_loaded{s}{h}") for h in range(2)] for s in range(2)]
        max_mm, max_red, m1_done, m2_done = sem("max_mm"), sem("max_red"), sem("m1_done"), sem("m2_done")
        max_tr, max_copied = sem("max_tr"), sem("max_copied")
        max_loaded = [sem("max_loaded0"), sem("max_loaded1")]
        sc_mm, exp_done, pv_mm = sem("sc_mm"), sem("exp_done"), sem("pv_mm")
        o_copied, o_tr, recip_done, o_normed = sem("o_copied"), sem("o_tr"), sem("recip_done"), sem("o_normed")
        ot_mm, ot_high_done, ot_low_done, out_mm = (
            sem("ot_mm"), sem("ot_high_done"), sem("ot_low_done"), sem("out_mm"))
        xb_done, xmid_done, stat_done, aggr_done = (
            sem("xb_done"), sem("xmid_done"), sem("stat_done"), sem("aggr_done"))
        xn_done, xt_mm, xt_high_done, xt_low_done = (
            sem("xn_done"), sem("xt_mm"), sem("xt_high_done"), sem("xt_low_done"))
        xmid_stored = [sem("xmid_stored0"), sem("xmid_stored1")]
        eb_loaded, g_mm, g_relu_done, g_part = sem("eb_loaded"), sem("g_mm"), sem("g_relu_done"), sem("g_part")
        g_sum, g_gate_mm, g_t_done, g_exp_mm = sem("g_sum"), sem("g_gate_mm"), sem("g_t_done"), sem("g_exp_mm")
        g_row_done, g_stored, gates_loaded = sem("g_row_done"), sem("g_stored"), sem("gates_loaded")
        acc_loaded = [sem(f"acc_loaded{t}") for t in range(TT)]
        y_loaded, y_ready = sem("y_loaded"), sem("y_ready")
        raw_loaded = [sem("raw_loaded0"), sem("raw_loaded1")]
        wh_done, wl_done = sem("wh_done"), sem("wl_done")
        z1_mm, acc_done = sem("z1_mm"), sem("acc_done")
        h_tr, h_high_done, h_low_done = sem("h_tr"), sem("h_high_done"), sem("h_low_done")
        z2_mm, y_done, out_stored = sem("z2_mm"), sem("y_done"), sem("out_stored")

        def three(pe, out_ap, left, right, tiles, stop_last=True):
            n = 0
            for a, b in ((0, 0), (0, 1), (1, 0)):
                for k in range(tiles):
                    last = pe.matmul(out_ap, left(a, k), right(b, k), start=(n == 0), stop=(n == 3 * tiles - 1))
                    n += 1
            return last

        L1N = 2 * E
        L2P = E // 2
        L2C = OT // 2
        NB1 = 7

        block = stack.enter_context(nc.Block())

        @block.sync
        def _(sp):
            sp.dma_start(x_all[:, 0:GB, :], x[0:GB].rearrange("b q c -> q b c")).then_inc(x_loaded[0], 16)
            sp.dma_start(w_f32[:, WQ], wq).then_inc(wq_loaded, 16)
            for g in range(1, NG):
                sp.dma_start(x_all[:, GB * g:GB * g + GB, :],
                             x[GB * g:GB * g + GB].rearrange("b q c -> q b c")).then_inc(x_loaded[g], 16)
            for dst, src in ((bq_sb, bq), (bk_sb, bk), (bv_sb, bv), (gb1_sb, gb1), (gb2_sb, gb2), (gw2_sb, gw2)):
                sp.dma_start(dst[:], src).then_inc(small_loaded, 16)
            sp.dma_start(bo_row[:], bo.to_broadcast([NQ, C])).then_inc(small_loaded, 16)
            for n, w in ((WK, wk), (WV, wv), (WO, wo), (GW1, gw1)):
                sp.dma_start(w_f32[:, n], w).then_inc(w_loaded, 16)

            for n in range(2):
                sp.dma_start(w_raw[:, n], w1[n]).then_inc(raw_loaded[n], 16)

            def load_context(b):
                if not b.exists:
                    return
                need(sp, c_high_done, b.times(1, -1))
                need(sp, c_low_done, b.times(1, -1))
                dram = ctx_t[:, b.times(1), :, :] if b.i is None else ctx_t[:, bass.ds(b.times(1), 1), :, :]
                sp.dma_start(c_raw[:, b.slot, :, 0:NKV], dram).then_inc(c_loaded[b.slot], 16)

            sp.wait_ge(pad_set, 1)
            load_context(Batch(0))

            for g in range(NG):
                sp.wait_ge(q3_done, g + 1)
                for j in range(GB):
                    sp.dma_start(
                        q_dram[GB * g + j].rearrange("p d (h t) -> (d h) p t", h=HH),
                        q_parts[:, :, j].rearrange("p k m t -> p k (m t)")).then_inc(q_stored, 16)
                if g < NG - 1:
                    continue
                sp.wait_ge(q_stored, 16 * B)

            def load_queries(b, h):
                need(sp, sc_mm, b.times(6, -12 + 3 * (h + 1)))
                cols = slice(h * HH * NQ, (h + 1) * HH * NQ)
                q = q_dram[b.times(1)] if b.i is None else q_dram[bass.ds(b.times(1), 1)].rearrange("a p d t -> (a p) d t")
                for row, part, reps in ((0, 0, 3), (3 * D, 1, 2), (5 * D, 2, 1)):
                    src = q[part:part + 1, :, cols].to_broadcast([reps, D, HH * NQ])
                    sp.dma_start(q_stack[row:row + reps * D, b.slot, cols], src).then_inc(stack_loaded[b.slot][h], 16)

            def load_keys(b, h):
                need(sp, k_stored, b.times(16, 16))
                need(sp, sc_mm, b.times(6, -12 + 3 * (h + 1)))
                k = k_dram[b.slot]
                for row, parts in ((0, 3), (3 * D, 2), (5 * D, 1)):
                    sp.dma_start(
                        k_stack[row:row + parts * D, b.slot, h * HH:(h + 1) * HH, :].rearrange("p h t -> p (h t)"),
                        k[0:parts, :, h * HH * KVP:(h + 1) * HH * KVP].rearrange("p d t -> (p d) t"),
                    ).then_inc(stack_loaded[b.slot][h], 16)

            def load_maxima(b, h):
                need(sp, max_copied, b.times(2, h + 1))
                sp.dma_start(q_stack[QROWS:SROWS, b.slot, h * HH * NQ:(h + 1) * HH * NQ],
                             max_rows[:, h, :]).then_inc(max_loaded[h], 16)

            def step(s):
                if (s + -2).exists:
                    b = s + -2
                    need(sp, xmid_done, b.times(1, 1))
                    dst = xmid_dram.rearrange("(b q) c -> b q c", q=NQ)
                    dst = dst[b.times(1)] if b.i is None else dst[bass.ds(b.times(1), 1)].rearrange("a q c -> (a q) c")
                    sp.dma_start(dst, x_mid[:, b.slot, :]).then_inc(xmid_stored[b.slot], 16)
                load_context(s + 4)
                if s.exists:
                    load_maxima(s, 1)
                if (s + 2).exists:
                    load_queries(s + 2, 0)
                if (s + 1).exists:
                    load_maxima(s + 1, 0)
                if (s + 2).exists:
                    b = s + 2
                    need(sp, sc_mm, b.times(6, -12 + 4))
                    need(sp, k3_done, b.times(1, 1))
                    sp.dma_start(k_dram[b.slot].rearrange("p d (h t) -> (d h) p t", h=HH),
                                 k_parts[:].rearrange("p k m t -> p k (m t)")).then_inc(k_stored, 16)
                    load_keys(b, 0)
                    load_queries(b, 1)
                    load_keys(b, 1)

            steps(sp, step)

            sp.wait_ge(c_low_done, B)
            sp.wait_ge(v_mm, CH * B)
            sp.wait_ge(ident_set, 3)
            sp.dma_start(eb_sb[:, 0:DFF + C], eb).then_inc(eb_loaded, 16)
            sp.dma_start(eb_sb[:, DFF + C:GCOLS], ident_e[:]).then_inc(eb_loaded, 16)

            def load_raw(freed, slot, src):
                sp.wait_ge(wl_done, freed)
                sp.dma_start(w_raw[:, slot], src).then_inc(raw_loaded[slot], 16)

            for n in range(2):
                load_raw(n + 1, n, w1[2 + n])

            sp.wait_ge(g_row_done, 3)
            for n in range(2):
                sp.dma_start(gate_dram[n * NQ:(n + 1) * NQ], g_row[:]).then_inc(g_stored, 16)
            sp.wait_ge(g_stored, 32)

            def gate_rows(t):
                p = t % PAT
                return gate_dram[16 * p:16 * p + P]

            sp.dma_start(acc[:, 0, :], gate_rows(0)[:, 0:DFF]).then_inc(acc_loaded[0], 16)
            for p in range(PAT):
                sp.dma_start(gates[:, p, :], gate_rows(p)[:, DFF:GCOLS]).then_inc(gates_loaded, 16)
            for t in range(1, TT):
                sp.dma_start(acc[:, t, :], gate_rows(t)[:, 0:DFF]).then_inc(acc_loaded[t], 16)
            for s in range(2):
                sp.wait_ge(xmid_stored[s], 16 * B // 2)
            sp.dma_start(y[:], xmid_dram.rearrange("(t p) c -> p t c", p=P)).then_inc(y_loaded, 16)

            with sp.Fori(2, E) as e:
                for n in range(2):
                    load_raw(e * 2 + (n - 1), n, w1[bass.ds(e * 2 + n, 1)].rearrange("a p k n -> (a p) k n"))
            with sp.Fori(0, L2P) as ep:
                for c in range(L2C):
                    load_raw(ep * L2C + (L1N + c - 1), c % 2,
                             w2[bass.ds(ep * L2C + c, 1)].rearrange("a p k n -> (a p) k n"))

            outs = out.rearrange("(t p) c -> t p c", p=P)
            for t in range(TT):
                sp.wait_ge(y_done, 2 * (TT * (L2P - 1) + t + 1))
                sp.dma_start(outs[t], y[:, t, :]).then_inc(out_stored, 16)
            sp.wait_ge(out_stored, 16 * TT)

        @block.gpsimd
        def _(pool):
            pool.memset(c_raw[:, :, :, NKV:KVE], 0.0).then_inc(pad_set, 1)
            pool.memset(ident[:], 0.0).then_inc(zero_set, 1)
            pool.memset(ident_b[:], 0.0).then_inc(zero_set, 1)
            pool.memset(ident_e[:], 0.0).then_inc(zero_set, 1)
            pool.wait_ge(zero_set, 3)
            for m, n in ((ident, P), (ident_b, P), (ident_e, E)):
                pool.affine_select(out=m[:], in_=m[:], compare_op=ALU.not_equal, fill=1.0, base=0,
                                   pattern=[[-1, n]], channel_multiplier=1).then_inc(ident_set, 1)
            pool.memset(magic[:], MAGIC)
            pool.memset(one_half[:], 1.5).then_inc(root_set, 1)
            pool.wait_ge(root_set, 1)
            pool.memset(k_parts[:, :, :, KVE:KVP], 0.0).then_inc(ones_set, 1)
            pool.memset(v_ones[:, :, :, :, D:VW], 1.0).then_inc(ones_set, 1)

            def inverse_root(n, before):
                y, t = rstd[:, 0:n], root_tmp[:, 0:n]
                pool.tensor_tensor(y.bitcast(I32), magic[:, 0:n], half_bits[:, 0:n], ALU.subtract).then_inc(root_done, 1)
                for k in range(ROOT_STEPS):
                    pool.wait_ge(root_done, before + (4 * k + 1))
                    pool.tensor_tensor(t, y, y, ALU.mult).then_inc(root_done, 1)
                    pool.wait_ge(root_done, before + (4 * k + 2))
                    pool.tensor_tensor(t, t, half_var[:, 0:n], ALU.mult).then_inc(root_done, 1)
                    pool.wait_ge(root_done, before + (4 * k + 3))
                    pool.tensor_tensor(t, one_half[:, 0:n], t, ALU.subtract).then_inc(root_done, 1)
                    pool.wait_ge(root_done, before + (4 * k + 4))
                    pool.tensor_tensor(y, y, t, ALU.mult).then_inc(root_done, 1)

            for g in range(NG):
                pool.wait_ge(bits_halved, g + 1)
                need(pool, q_norm, GB * g)
                inverse_root(GB, ROOT_OPS * g)

            pool.wait_ge(q_stored, 16 * B)
            pool.memset(k_stack[QROWS:SROWS, :, :, :], -1.0).then_inc(stack_set, 1)
            pool.wait_ge(stack_set, 1)

            def step(s):
                b = s + -1
                if b.exists:
                    need(pool, bias_done, 1) if b.i is None and b.c == 0 else None
                    need(pool, xmid_done, b.times(1, 0))
                    src = x_all[:, b.times(1), :] if b.i is None else x_all[:, bass.ds(b.times(1), 1), :]
                    pool.tensor_tensor(x_bias[:], src, bias_row[:], ALU.add).then_inc(xb_done, 1)
                b = s + -2
                if b.exists:
                    need(pool, bits_halved, b.times(1, 1) + NG)
                    inverse_root(1, b.times(ROOT_OPS) + ROOT_OPS * NG)
                b = s + 2
                if b.exists:
                    need(pool, k1_done, b.times(1, 1))
                    pool.tensor_tensor(k_rest[:], k_f32[:], k_parts[:, 0, :, 0:KVE], ALU.subtract)\
                        .then_inc(kr_done, 1)
                b = s + 3
                if b.exists:
                    need(pool, c_high_done, b.times(1, 1))
                    pool.tensor_tensor(c_low[:, b.slot], c_raw[:, b.slot], c_high[:, b.slot], ALU.subtract)\
                        .then_inc(c_low_done, 1)

            steps(pool, step)

            def low_part(r, slot, dst):
                pool.wait_ge(wh_done, r)
                pool.tensor_tensor(dst(1), w_raw[:, slot], dst(0), ALU.subtract).then_inc(wl_done, 1)

            for s in range(2):
                low_part(s + 1, s, lambda part: w1_parts[:, s, part])
            pool.wait_ge(y_loaded, 16)
            pool.wait_ge(gates_loaded, 16 * PAT)
            for n in range(TT // PAT):
                rows = slice(n * PAT, (n + 1) * PAT)
                pool.tensor_tensor(y[:, rows, :], y[:, rows, :], gates[:, :, 0:C], ALU.add).then_inc(y_ready, 1)
            with pool.Fori(1, E) as e:
                for s in range(2):
                    low_part(e * 2 + s + 1, s, lambda part: w1_parts[:, s, part])
            with pool.Fori(0, L2P) as ep:
                for c in range(L2C):
                    low_part(ep * L2C + (L1N + c + 1), c % 2,
                             lambda part: w2_parts[:, bass.ds(ep % 2, 1), c, part].rearrange("p s a n -> p (s a) n"))

        @block.scalar
        def _(act):
            act.wait_ge(wq_loaded, 16)
            act.activation(w_high[:, WQ], w_f32[:, WQ], ACT.Copy).then_inc(w_high_done, 1)
            act.wait_ge(small_loaded, 16 * 7)
            for g in range(NG):
                act.wait_ge(q_tr, g + 1)
                need(act, q_mm, 2 * g)
                act.activation(xqt_high[:], ps_sc[:, 0:2, 0:GW], ACT.Copy).then_inc(q_xhigh, 1)
                if g == 0:
                    act.wait_ge(w_loaded, 16 * 4)
                    act.activation(w_high[:, WK:GW1 + 1], w_f32[:, WK:GW1 + 1], ACT.Copy).then_inc(w_high_done, 1)
                need(act, q3_done, g)
                for m in range(2):
                    act.wait_ge(q_mm, 2 * g + m + 1)
                    act.activation(q_f32[:, :, m, :], ps_sc[:, 2 + m, 0:GW].rearrange("p (b t) -> p b t", b=GB),
                                   ACT.Identity, bias=bq_sb[:, m:m + 1]).then_inc(q_evac, 1)

            def exp(b, p):
                if not b.exists:
                    return
                need(act, sc_mm, b.times(6, p + 1))
                need(act, pv_mm, b.times(2, -2 + p // CH + 1))
                act.activation(probs[:, p], ps_sc[:, 2 * (p % 2):2 * (p % 2) + 2, 0:4 * NQ], ACT.Exp,
                               scale=SCALE).then_inc(exp_done, 1)

            def key_evac(b, m):
                if b.exists:
                    need(act, k_mm, b.times(2, m + 1))
                    need(act, kr_done, b.times(1, 0))
                    act.activation(k_f32[:, m, :], ps_w[:, 0:KVE], ACT.Identity, bias=bk_sb[:, m:m + 1])\
                        .then_inc(k_evac, 1)

            def value_evac(b, c):
                if b.exists:
                    n = CHROWS[c]
                    need(act, v_mm, b.times(3, c + 1))
                    need(act, pv_mm, b.times(2, -2))
                    act.activation(v_ones[0:n, b.slot, c, :, 0:D],
                                   ps_w[0:n, 0:C].rearrange("p (h d) -> p h d", h=H), ACT.Copy).then_inc(v_evac, 1)

            def max_copy(b, h):
                if b.exists:
                    need(act, max_tr, b.times(2, h + 1))
                    need(act, max_loaded[h], b.times(16))
                    act.activation(max_rows[:, h, :], ps_max_t, ACT.Copy).then_inc(max_copied, 1)

            def step(s):
                exp(s, 0)
                key_evac(s + 2, 0)
                max_copy(s, 1)
                exp(s, 1)
                key_evac(s + 2, 1)
                b = s + -1
                if b.exists:
                    need(act, pv_mm, b.times(2, 2))
                    need(act, o_tr, b.times(1))
                    act.activation(o_full[:], ps_o[:, 0:4 * NQ], ACT.Copy).then_inc(o_copied, 1)
                value_evac(s + 1, 0)
                exp(s, 2)
                value_evac(s + 1, 1)
                value_evac(s + 1, 2)
                exp(s, 3)
                b = s + 3
                if b.exists:
                    need(act, c_loaded[b.slot], b.uses(16))
                    need(act, v_mm, b.times(3, -3))
                    act.activation(c_high[:, b.slot], c_raw[:, b.slot], ACT.Copy).then_inc(c_high_done, 1)
                max_copy(s + 1, 0)
                b = s + -1
                if b.exists:
                    need(act, ot_mm, b.times(1, 1))
                    act.activation(ot_high[:], ps_w[:, 0:2 * NQ].rearrange("p (a t) -> p a t", a=2), ACT.Copy)\
                        .then_inc(ot_high_done, 1)
                exp(s, 4)
                b = s + -2
                if b.exists:
                    need(act, xt_mm, b.times(1, 1))
                    at = b.times(NQ)
                    dst = xt_parts[:, 0, :, at:at + NQ] if b.i is None else xt_parts[:, 0, :, bass.ds(at, NQ)]
                    act.activation(dst, ps_w[:, 0:2 * NQ].rearrange("p (a t) -> p a t", a=2), ACT.Copy)\
                        .then_inc(xt_high_done, 1)
                exp(s, 5)

            act.wait_ge(pad_set, 1)
            steps(act, step)

            def high_part(loaded, slot, dst):
                act.wait_ge(raw_loaded[slot], loaded)
                act.activation(dst, w_raw[:, slot], ACT.Copy).then_inc(wh_done, 1)

            for s in range(2):
                high_part(16, s, w1_parts[:, s, 0])

            for g in range(NG):
                for m in range(2):
                    n = 2 * g + m
                    act.wait_ge(g_mm, n + 1)
                    need(act, g_part, n - 1)
                    act.activation(g_relu[:, m, :], banks[:, m, 0:GW], ACT.Relu, bias=gb1_sb[:, m:m + 1])\
                        .then_inc(g_relu_done, 1)
            act.wait_ge(g_gate_mm, 1)
            act.activation(gate_t[:], banks[0:E, 2, 0:NQ], ACT.Identity, bias=gb2_sb[:, 0:1], scale=1.0 / B)\
                .then_inc(g_t_done, 1)
            for n in range(3):
                cols = slice(512 * n, min(512 * (n + 1), GCOLS))
                act.wait_ge(g_exp_mm, n + 1)
                act.activation(g_row[:, cols], banks[0:NQ, 3 + n, 0:cols.stop - cols.start], ACT.Copy)\
                    .then_inc(g_row_done, 1)

            with act.Fori(1, E) as e:
                for s in range(2):
                    act.wait_ge(z1_mm, e * (2 * TT) + (s - 1) * TT)
                    high_part(e * 16 + 16, s, w1_parts[:, s, 0])
            for c in range(L2C):
                if c >= 2:
                    act.wait_ge(z1_mm, TT * (L1N - 3 + c))
                high_part(16 * (E + c // 2 + 1), c % 2, w2_parts[:, 0, c, 0])
            for t in range(TT):
                act.wait_ge(h_tr, t + 1)
                act.activation(h_high[:, t], banks[:, 4 + 2 * (t % 2):6 + 2 * (t % 2), :], ACT.Relu)\
                    .then_inc(h_high_done, 1)
                if t == 1:
                    for c in range(L2C):
                        high_part(16 * (E + 2 + c // 2 + 1), c % 2, w2_parts[:, 1, c, 0])
            with act.Fori(2, L2P) as ep:
                act.wait_ge(z2_mm, ep * TT - TT)
                for c in range(L2C):
                    high_part(ep * 32 + 16 * (E + c // 2 + 1), c % 2,
                              w2_parts[:, bass.ds(ep % 2, 1), c, 0].rearrange("p s a n -> p (s a) n"))

        @block.vector
        def _(dve):
            def halve_bits(n, aggregated, count):
                value, of = aggregated
                dve.wait_ge(of, value)
                dve.tensor_scalar(half_var[:, 0:n], mean_var[:, 0:n, 1], EPS, 0.5, ALU.add, ALU.mult)\
                    .then_inc(eps_added, 1)
                dve.wait_ge(eps_added, count)
                dve.tensor_scalar(half_bits[:, 0:n], half_var[:, 0:n].bitcast(I32), 1, None,
                                  ALU.logical_shift_right).then_inc(bits_halved, 1)

            for g in range(NG):
                dve.wait_ge(x_loaded[g], 16)
                need(dve, root_done, ROOT_OPS * g)
                for j in range(GB):
                    dve.bn_stats(stats[:, j, :], x_all[:, GB * g + j, :]).then_inc(q_stat, 1)
                for j in range(GB):
                    dve.wait_ge(q_stat, GB * g + j + 1)
                    dve.bn_aggr(mean_var[:, j, :], stats[:, j, :]).then_inc(q_aggr, 1)
                if g == 0:
                    dve.wait_ge(w_high_done, 1)
                    dve.tensor_tensor(w_low[:, WQ], w_f32[:, WQ], w_high[:, WQ], ALU.subtract).then_inc(w_low_done, 1)
                halve_bits(GB, (GB * (g + 1), q_aggr), g + 1)
                dve.wait_ge(root_done, ROOT_OPS * (g + 1))
                need(dve, q_tr, g)
                for j in range(GB):
                    dve.tensor_scalar(xq[:, j, :], x_all[:, GB * g + j, :], mean_var[:, j, 0:1], rstd[:, j:j + 1],
                                      ALU.subtract, ALU.mult).then_inc(q_norm, 1)
                dve.wait_ge(q_xhigh, g + 1)
                dve.tensor_tensor(xqt_low[:], ps_sc[:, 0:2, 0:GW], xqt_high[:], ALU.subtract).then_inc(q_xlow, 1)
                if g == 0:
                    dve.wait_ge(small_loaded, 16 * 7)
                    dve.tensor_copy(bv_wide[:], bv_sb[:].unsqueeze(2).to_broadcast([P, 2, NQ])).then_inc(bv_wide_done, 1)
                    dve.wait_ge(w_high_done, 2)
                    dve.tensor_tensor(w_low[:, WK:GW1 + 1], w_f32[:, WK:GW1 + 1], w_high[:, WK:GW1 + 1],
                                      ALU.subtract).then_inc(w_low_done, 1)
                dve.wait_ge(q_evac, 2 * (g + 1))
                need(dve, q_stored, 16 * GB * g)
                dve.tensor_copy(q_parts[:, 0], q_f32[:]).then_inc(q1_done, 1)
                dve.wait_ge(q1_done, g + 1)
                dve.tensor_tensor(q_rest[:], q_f32[:], q_parts[:, 0], ALU.subtract).then_inc(qr_done, 1)
                dve.wait_ge(qr_done, g + 1)
                dve.tensor_copy(q_parts[:, 1], q_rest[:]).then_inc(q2_done, 1)
                dve.wait_ge(q2_done, g + 1)
                dve.tensor_tensor(q_parts[:, 2], q_rest[:], q_parts[:, 1], ALU.subtract).then_inc(q3_done, 1)

            dve.wait_ge(bias_mm, 1)
            dve.tensor_tensor(bias_row[:], ps_o[0:NQ, 0:C], bo_row[:], ALU.add).then_inc(bias_done, 1)

            def reduce_max(b, k):
                if b.exists:
                    need(dve, max_mm, b.times(8, k + 1))
                    dve.tensor_reduce(maxima[:, b.slot, 2 * k:2 * k + 2], ps_max[0:NQ, :, 0:NKV], AX_X, ALU.max)\
                        .then_inc(max_red, 1)

            def max_first(b, h):
                if b.exists:
                    need(dve, max_red, b.times(8, 4 * h + 4))
                    need(dve, max_tr, b.times(2, h - 1))
                    dve.tensor_copy(max_parts[:, h, 0, :], maxima[:, b.slot, HH * h:HH * h + HH]).then_inc(m1_done, 1)

            def max_second(b, h):
                if b.exists:
                    need(dve, m1_done, b.times(2, h + 1))
                    dve.tensor_tensor(max_parts[:, h, 1, :], maxima[:, b.slot, HH * h:HH * h + HH],
                                      max_parts[:, h, 0, :], ALU.subtract).then_inc(m2_done, 1)

            def step(s):
                old, last, new = s + -2, s + -1, s + 2
                max_first(s, 1)
                if old.exists:
                    need(dve, out_mm, old.times(1, 1))
                    need(dve, xb_done, old.times(1, 1))
                    need(dve, xmid_stored[old.slot], old.uses(16) + -16)
                    dve.tensor_tensor(x_mid[:, old.slot, :], ps_w[0:NQ, 0:C], x_bias[:], ALU.add).then_inc(xmid_done, 1)
                max_second(s, 1)
                if old.exists:
                    need(dve, xmid_done, old.times(1, 1))
                    dve.bn_stats(stats[:, 0, :], x_mid[:, old.slot, :]).then_inc(stat_done, 1)
                if old.exists:
                    need(dve, stat_done, old.times(1, 1))
                reduce_max(s + 1, 0)
                if old.exists:
                    dve.bn_aggr(mean_var[:, 0, :], stats[:, 0, :]).then_inc(aggr_done, 1)
                reduce_max(s + 1, 1)
                if old.exists:
                    halve_bits(1, (old.times(1, 1), aggr_done), old.times(1, 1) + NG)
                if new.exists:
                    need(dve, k_evac, new.times(2, 2))
                    need(dve, k_stored, new.times(16))
                    dve.tensor_copy(k_parts[:, 0, :, 0:KVE], k_f32[:]).then_inc(k1_done, 1)
                reduce_max(s + 1, 2)
                reduce_max(s + 1, 3)
                if old.exists:
                    need(dve, root_done, old.times(ROOT_OPS, ROOT_OPS) + ROOT_OPS * NG)
                    dve.tensor_scalar(x_norm[:], x_mid[:, old.slot, :], mean_var[:, 0, 0:1], rstd[:, 0:1],
                                      ALU.subtract, ALU.mult).then_inc(xn_done, 1)
                max_first(s + 1, 0)
                if last.exists:
                    need(dve, o_tr, last.times(1, 1))
                    sums = ps_o[0:NQ, :].rearrange("p (h w) -> p h w", w=VW)
                    dve.reciprocal(recip[:], sums[:, :, D]).then_inc(recip_done, 1)
                max_second(s + 1, 0)
                if last.exists:
                    need(dve, recip_done, last.times(1, 1))
                    dve.tensor_tensor(o_norm[:], sums[:, :, 0:D], recip[:].unsqueeze(2).to_broadcast([NQ, H, D]),
                                      ALU.mult).then_inc(o_normed, 1)
                reduce_max(s + 1, 4)
                if new.exists:
                    need(dve, kr_done, new.times(1, 1))
                    dve.tensor_copy(k_parts[:, 1, :, 0:KVE], k_rest[:]).then_inc(k2_done, 1)
                reduce_max(s + 1, 5)
                if new.exists:
                    need(dve, k2_done, new.times(1, 1))
                    dve.tensor_tensor(k_parts[:, 2, :, 0:KVE], k_rest[:], k_parts[:, 1, :, 0:KVE], ALU.subtract)\
                        .then_inc(k3_done, 1)
                if last.exists:
                    need(dve, ot_high_done, last.times(1, 1))
                    dve.tensor_tensor(ot_low[:], ps_w[:, 0:2 * NQ].rearrange("p (a t) -> p a t", a=2), ot_high[:],
                                      ALU.subtract).then_inc(ot_low_done, 1)
                reduce_max(s + 1, 6)
                if old.exists:
                    need(dve, xt_high_done, old.times(1, 1))
                    at = old.times(NQ)
                    cols = slice(at, at + NQ) if old.i is None else bass.ds(at, NQ)
                    dve.tensor_tensor(xt_parts[:, 1, :, cols], ps_w[:, 0:2 * NQ].rearrange("p (a t) -> p a t", a=2),
                                      xt_parts[:, 0, :, cols], ALU.subtract).then_inc(xt_low_done, 1)
                reduce_max(s + 1, 7)

            dve.wait_ge(ones_set, 1)
            steps(dve, step)

            for g in range(NG):
                for m in range(2):
                    dve.wait_ge(g_relu_done, 2 * g + m + 1)
                    dve.tensor_reduce(h_sums[:, m, g, :], g_relu[:, m, :].rearrange("p (b t) -> p t b", b=GB),
                                      AX_X, ALU.add).then_inc(g_part, 1)
            dve.wait_ge(g_part, 2 * NG)
            dve.tensor_reduce(h_sum[:], h_sums[:].rearrange("p m g t -> p m t g"), AX_X, ALU.add).then_inc(g_sum, 1)

            dve.wait_ge(gates_loaded, 16 * PAT)

            def add_first(e, s, t):
                dve.wait_ge(z1_mm, e * (2 * TT) + (s * TT + t + 1))
                gate_col = gates[:, t % PAT, C + e:C + e + 1] if isinstance(e, int) else \
                    gates[:, t % PAT, bass.ds(e + C, 1)]
                dve.scalar_tensor_tensor(out=acc[:, t, 512 * s:512 * s + 512], in0=banks[:, t % NB1, :],
                                         scalar=gate_col, in1=acc[:, t, 512 * s:512 * s + 512],
                                         op0=ALU.mult, op1=ALU.add).then_inc(acc_done, 1)

            for s in range(2):
                for t in range(TT):
                    if s == 0:
                        dve.wait_ge(acc_loaded[t], 16)
                    add_first(0, s, t)
            with dve.Fori(1, E) as e:
                for s in range(2):
                    for t in range(TT):
                        add_first(e, s, t)

            def add_second(ep, t):
                dve.wait_ge(z2_mm, ep * TT + (t + 1))
                for k in range(2):
                    gate_col = gates[:, t % PAT, C + 2 * ep + k:C + 2 * ep + k + 1] if isinstance(ep, int) else \
                        gates[:, t % PAT, bass.ds(ep * 2 + (C + k), 1)]
                    if k == 1:
                        dve.wait_ge(y_done, ep * (2 * TT) + (2 * t + 1))
                    dve.scalar_tensor_tensor(out=y[:, t, :], in0=banks[:, t % 2, C * k:C * k + C], scalar=gate_col,
                                             in1=y[:, t, :], op0=ALU.mult, op1=ALU.add).then_inc(y_done, 1)

            def hidden_low(t):
                dve.wait_ge(h_high_done, t + 1)
                ps = banks[:, 4 + 2 * (t % 2):6 + 2 * (t % 2), :].rearrange("p k n -> p (k n)")
                dve.scalar_tensor_tensor(out=h_low[:, t].rearrange("p k n -> p (k n)"), in0=ps, scalar=0.0,
                                         in1=h_high[:, t].rearrange("p k n -> p (k n)"),
                                         op0=ALU.max, op1=ALU.subtract).then_inc(h_low_done, 1)

            dve.wait_ge(y_ready, TT // PAT)
            hidden_low(0)
            for t in range(TT):
                if t + 1 < TT:
                    hidden_low(t + 1)
                add_second(0, t)
            with dve.Fori(1, L2P) as ep:
                for t in range(TT):
                    add_second(ep, t)

        @block.tensor
        def _(pe):
            pe.wait_ge(ident_set, 3)
            for g in range(NG):
                pe.wait_ge(q_norm, GB * (g + 1))
                need(pe, q_xlow, g)
                for j in range(GB):
                    for k in range(IT):
                        last = pe.transpose(ps_sc[:, k, j * NQ:(j + 1) * NQ], xq[:, j, P * k:P * k + P],
                                            ident[0:NQ, 0:NQ])
                last.then_inc(q_tr, 1)
                pe.wait_ge(q_xlow, g + 1)
                if g == 0:
                    pe.wait_ge(w_low_done, 1)
                need(pe, q_evac, 2 * g)
                xqt = (xqt_high, xqt_low)
                w_part = (w_high, w_low)
                for m in range(2):
                    three(pe, ps_sc[:, 2 + m, 0:GW], lambda a, k: w_part[a][:, WQ, k, P * m:P * m + P],
                          lambda a, k: xqt[a][:, k, :], IT).then_inc(q_mm, 1)
            pe.wait_ge(w_low_done, 2)
            pe.wait_ge(bv_wide_done, 1)
            for k in range(IT):
                last = pe.matmul(ps_o[0:NQ, 0:C], bv_wide[:, k, :], w_f32[:, WO, k, :], start=(k == 0), stop=(k == 1))
            last.then_inc(bias_mm, 1)
            pe.wait_ge(q_evac, 2 * NG)
            pe.wait_ge(bias_done, 1)
            pe.wait_ge(ones_set, 2)

            c_part = (c_high, c_low)

            def key_project(b, m):
                if not b.exists:
                    return
                if m == 0:
                    need(pe, c_low_done, b.times(1, 1))
                    need(pe, xmid_done, b.times(1, -3))
                    if b.i is None and b.c < 4:
                        need(pe, v_evac, b.times(3, -3))
                else:
                    need(pe, k_evac, b.times(2, 1))
                three(pe, ps_w[:, 0:KVE], lambda a, k: w_part[a][:, WK, k, P * m:P * m + P],
                      lambda a, k: c_part[a][:, b.slot, k, :], IT).then_inc(k_mm, 1)

            def value_project(b, c):
                if not b.exists:
                    return
                n = CHROWS[c]
                if c == 0:
                    need(pe, k_evac, (b + 1).times(2, 2))
                    if b.i is None and b.c == B - 1:
                        need(pe, xmid_done, b.times(1, -2))
                else:
                    need(pe, v_evac, b.times(3, c))
                three(pe, ps_w[0:n, 0:C], lambda a, k: c_part[a][:, b.slot, k, P * c:P * c + n],
                      lambda a, k: w_part[a][:, WV, k, :], IT).then_inc(v_mm, 1)

            def max_scores(b, k):
                if not b.exists:
                    return
                if k % 4 == 0:
                    need(pe, stack_loaded[b.slot][k // 4], b.uses(96))
                need(pe, max_red, b.times(8, k))
                if k == 1:
                    need(pe, max_copied, b.times(2))
                if k == 5:
                    need(pe, max_copied, b.times(2, 1))
                for n in range(2):
                    h = 2 * k + n
                    last = pe.matmul(ps_max[0:NQ, n, 0:NKV], q_stack[0:QROWS, b.slot, h * NQ:(h + 1) * NQ],
                                     k_stack[0:QROWS, b.slot, h, 0:NKV], start=True, stop=True)
                last.then_inc(max_mm, 1)

            def max_transpose(b, h):
                if not b.exists:
                    return
                need(pe, m2_done, b.times(2, h + 1))
                need(pe, max_red, b.times(8, 9 if h else 5))
                pe.transpose(ps_max_t, max_parts[:, h].rearrange("p a h -> p (a h)"), ident_b[0:NQ, 0:NQ])\
                    .then_inc(max_tr, 1)

            def scores(b, p):
                if not b.exists:
                    return
                h, c = p // CH, p % CH
                if c == 0:
                    need(pe, max_loaded[h], b.times(16, 16))
                need(pe, exp_done, b.times(6, p - 1))
                for n in range(HH):
                    head = HH * h + n
                    last = pe.matmul(ps_sc[:, 2 * (p % 2) + n // 4, (n % 4) * NQ:(n % 4 + 1) * NQ],
                                     k_stack[0:SROWS, b.slot, head, P * c:P * c + P],
                                     q_stack[0:SROWS, b.slot, head * NQ:(head + 1) * NQ], start=True, stop=True)
                last.then_inc(sc_mm, 1)

            def weigh_values(b, h):
                if not b.exists:
                    return
                need(pe, exp_done, b.times(6, CH * (h + 1)))
                if h == 0:
                    need(pe, v_evac, b.times(3, 3))
                    need(pe, o_normed, b.times(1))
                for hb in range(2 * h, 2 * h + 2):
                    for c in range(CH):
                        n = CHROWS[c]
                        for g in range(4):
                            last = pe.matmul(ps_o[VW * g:VW * g + VW, hb * NQ:(hb + 1) * NQ],
                                             v_ones[0:n, b.slot, c, 4 * hb + g, :],
                                             probs[0:n, CH * h + c, hb % 2, g * NQ:(g + 1) * NQ],
                                             start=(c == 0), stop=(c == CH - 1))
                last.then_inc(pv_mm, 1)

            def output_transpose(b):
                if not b.exists:
                    return
                need(pe, o_copied, b.times(1, 1))
                for hb in range(4):
                    last = pe.transpose(ps_o[0:NQ, P * hb:P * hb + P], o_full[:, hb * NQ:(hb + 1) * NQ], ident[:])
                last.then_inc(o_tr, 1)

            def output_back(b):
                if not b.exists:
                    return
                need(pe, o_normed, b.times(1, 1))
                need(pe, v_evac, (b + 2).times(3, 3))
                if b.i is None:
                    need(pe, xmid_done, b.times(1))
                for k in range(IT):
                    last = pe.transpose(ps_w[:, k * NQ:(k + 1) * NQ],
                                        o_norm[:, HH * k:HH * k + HH, :].rearrange("p h d -> p (h d)"),
                                        ident[0:NQ, 0:NQ])
                last.then_inc(ot_mm, 1)

            def output_project(b):
                if not b.exists:
                    return
                need(pe, ot_low_done, b.times(1, 1))
                need(pe, xt_low_done, b.times(1))
                ot = (ot_high, ot_low)
                three(pe, ps_w[0:NQ, 0:C], lambda a, k: ot[a][:, k, :], lambda a, k: w_part[a][:, WO, k, :], IT)\
                    .then_inc(out_mm, 1)

            def token_transpose(b):
                if not b.exists:
                    return
                need(pe, xn_done, b.times(1, 1))
                need(pe, ot_low_done, (b + 2).times(1))
                for k in range(IT):
                    last = pe.transpose(ps_w[:, k * NQ:(k + 1) * NQ], x_norm[:, P * k:P * k + P], ident[0:NQ, 0:NQ])
                last.then_inc(xt_mm, 1)

            def step(s):
                old, last, nxt, new = s + -2, s + -1, s + 1, s + 2
                max_scores(nxt, 0)
                scores(s, 0)
                key_project(new, 0)
                max_transpose(s, 1)
                scores(s, 1)
                key_project(new, 1)
                max_scores(nxt, 1)
                weigh_values(last, 1)
                value_project(nxt, 0)
                max_scores(nxt, 2)
                scores(s, 2)
                value_project(nxt, 1)
                max_scores(nxt, 3)
                output_transpose(last)
                value_project(nxt, 2)
                max_scores(nxt, 4)
                scores(s, 3)
                max_transpose(nxt, 0)
                output_back(last)
                scores(s, 4)
                max_scores(nxt, 5)
                weigh_values(s, 0)
                max_scores(nxt, 6)
                token_transpose(old)
                scores(s, 5)
                output_project(last)
                max_scores(nxt, 7)

            pe.wait_ge(stack_set, 1)
            steps(pe, step)

            for g in range(NG):
                for m in range(2):
                    n = 2 * g + m
                    need(pe, g_relu_done, n - 1)
                    if n == 0:
                        pe.wait_ge(xt_low_done, B)
                    three(pe, banks[:, m, 0:GW], lambda a, k: w_part[a][:, GW1, k, P * m:P * m + P],
                          lambda a, k: xt_parts[:, a, k, GW * g:GW * g + GW], IT).then_inc(g_mm, 1)
            pe.wait_ge(g_sum, 1)
            for k in range(2):
                last = pe.matmul(banks[0:E, 2, 0:NQ], gw2_sb[:, k, :], h_sum[:, k, :], start=(k == 0), stop=(k == 1))
            last.then_inc(g_gate_mm, 1)
            pe.wait_ge(g_t_done, 1)
            pe.wait_ge(eb_loaded, 32)
            for n in range(3):
                cols = slice(512 * n, min(512 * (n + 1), GCOLS))
                pe.matmul(banks[0:NQ, 3 + n, 0:cols.stop - cols.start], gate_t[:], eb_sb[:, cols],
                          start=True, stop=True).then_inc(g_exp_mm, 1)
            pe.wait_ge(g_row_done, 3)

            def first_layer(e, s, t, first):
                if t == 0:
                    pe.wait_ge(wl_done, e * 2 + (s + 1))
                if not (first and s * TT + t < NB1):
                    pe.wait_ge(acc_done, e * (2 * TT) + (s * TT + t - NB1 + 1))
                three(pe, banks[:, t % NB1, :], lambda a, k: xt_parts[:, a, k, P * t:P * t + P],
                      lambda a, k: w1_parts[:, s, a, k, :], IT).then_inc(z1_mm, 1)

            for s in range(2):
                for t in range(TT):
                    first_layer(0, s, t, True)
            with pe.Fori(1, E) as e:
                for s in range(2):
                    for t in range(TT):
                        first_layer(e, s, t, False)

            def hidden_transpose(t):
                pe.wait_ge(acc_done, 2 * TT * (E - 1) + TT + t + 1)
                if t < 2:
                    pe.wait_ge(acc_done, 2 * TT * E)
                else:
                    pe.wait_ge(h_low_done, t - 1)
                for k in range(OT):
                    last = pe.transpose(banks[:, 4 + 2 * (t % 2) + k // 4, P * (k % 4):P * (k % 4) + P],
                                        acc[:, t, P * k:P * k + P], ident[:])
                last.then_inc(h_tr, 1)

            h_part = (h_high, h_low)

            def second_layer(ep, slot, t, first):
                if first:
                    pe.wait_ge(h_low_done, t + 1)
                if not (first and t < 2):
                    pe.wait_ge(y_done, ep * (2 * TT) + 2 * (t - 1))
                n = 0
                for c in range(L2C):
                    if t == 0:
                        pe.wait_ge(wl_done, ep * L2C + (L1N + c + 1))
                    for a, b in ((0, 0), (0, 1), (1, 0)):
                        for k in range(2):
                            w = w2_parts[:, slot, c, b, k, :]
                            last = pe.matmul(banks[:, t % 2, :], h_part[a][:, t, 2 * c + k, :], w,
                                             start=(n == 0), stop=(n == 3 * OT - 1))
                            n += 1
                last.then_inc(z2_mm, 1)

            hidden_transpose(0)
            for t in range(TT):
                if t + 1 < TT:
                    hidden_transpose(t + 1)
                second_layer(0, 0, t, True)
            with pe.Fori(1, L2P) as ep:
                for t in range(TT):
                    second_layer(ep, bass.ds(ep % 2, 1), t, False)


def kernel(x, ctx_1024, L0_xattn_w_q, L0_xattn_b_q, L0_xattn_w_kv, L0_xattn_b_kv, L0_xattn_w_out, L0_xattn_b_out,
           L0_ffn_gW1, L0_ffn_gb1, L0_ffn_gW2, L0_ffn_gb2, L0_ffn_eW1, L0_ffn_eb1, L0_ffn_eW2, L0_ffn_eb2):
    import numpy as np
    import concourse.bacc as bacc
    from concourse.bass_utils import run_bass_kernel_spmd

    def a(v):
        return np.asarray(v)

    order = np.array([(2 * (p % HH) + m) * D + p // HH for m in range(2) for p in range(P)])
    w_kv, b_kv = a(L0_xattn_w_kv), a(L0_xattn_b_kv)

    def tiles(w):
        return w.reshape(IT, P, -1).transpose(1, 0, 2)

    e1, e2 = a(L0_ffn_eW1), a(L0_ffn_eW2)
    arrays = {
        "x": a(x),
        "ctx_t": a(ctx_1024).transpose(2, 0, 1).reshape(IT, P, B, NKV).transpose(1, 2, 0, 3),
        "wq": tiles(a(L0_xattn_w_q)[:, order]), "bq": a(L0_xattn_b_q)[order].reshape(2, P).T,
        "wk": tiles(w_kv[:, :C][:, order]), "bk": b_kv[:C][order].reshape(2, P).T,
        "wv": tiles(w_kv[:, C:]), "bv": b_kv[C:].reshape(2, P).T,
        "wo": tiles(a(L0_xattn_w_out)), "bo": a(L0_xattn_b_out).reshape(1, C),
        "gw1": tiles(a(L0_ffn_gW1).T), "gb1": a(L0_ffn_gb1).reshape(2, P).T,
        "gw2": a(L0_ffn_gW2).reshape(E, 2, P).transpose(2, 1, 0), "gb2": a(L0_ffn_gb2).reshape(E, 1),
        "w1": e1.reshape(E, 2, 512, IT, P).transpose(0, 1, 4, 3, 2).reshape(2 * E, P, IT, 512),
        "eb": np.concatenate([a(L0_ffn_eb1), a(L0_ffn_eb2)], axis=1),
        "w2": e2.reshape(E // 2, 2, C, OT // 2, 2, P).transpose(0, 3, 5, 4, 1, 2).reshape(2 * E, P, 2, 512),
    }
    arrays = {k: np.ascontiguousarray(v) for k, v in arrays.items()}
    nc = bacc.Bacc("TRN2", target_bir_lowering=False, num_devices=1)
    args = {k: nc.dram_tensor(f"in_{k}", v.shape, mybir.dt.from_np(v.dtype), kind="ExternalInput").ap()
            for k, v in arrays.items()}
    out = nc.dram_tensor("out", (T, C), F32, kind="ExternalOutput").ap()
    build(nc, out=out, **args)
    r = run_bass_kernel_spmd(nc, [{f"in_{k}": v for k, v in arrays.items()}], core_ids=[0])
    return r.results[0]["out"].reshape(B, NQ, C)
```

```python
from contextlib import ExitStack

import concourse.bass as bass
from concourse import mybir

F32 = mybir.dt.float32
F32R = mybir.dt.float32r
BF16 = mybir.dt.bfloat16
I32 = mybir.dt.int32
ALU = mybir.AluOpType
ACT = mybir.ActivationFunctionType
AX_X = mybir.AxisListType.X

P = 128
B, NQ, C = 16, 112, 256
NKV = 375
KVE = NKV + 1
KVP = 384
CH = KVP // P
CHROWS = [P, P, NKV - 2 * P]
H, D = 16, 16
HH = H // 2
HQ = H // 4
SCALE = float(D) ** -0.5
EPS = 1e-5
MAGIC = 0x5EF759DF
ROOT_STEPS = 3
ROOT_OPS = 1 + 4 * ROOT_STEPS
T = B * NQ
TT = T // P
PAT = NQ // 16
DFF, E = 1024, 8
IT = C // P
OT = DFF // P
GB = 4
NG = B // GB
GW = GB * NQ
VW = 2 * D
GCOLS = DFF + C + E
QROWS = 6 * D
SROWS = QROWS + 2


class Batch:

    def __init__(self, c, i=None):
        self.c, self.i = c, i

    def __add__(self, n):
        return Batch(self.c + n, self.i)

    @property
    def exists(self):
        return self.i is not None or 0 <= self.c < B

    @property
    def slot(self):
        return self.c % 2

    def times(self, per, more=0, of=B):
        if self.i is None:
            return min(per * self.c + more, per * of)
        return self.i * (2 * per) + (per * self.c + more)

    def uses(self, per):
        if self.i is None:
            return per * (self.c // 2 + 1)
        return self.i * per + per * (self.c // 2 + 1)


FIRST_STEP, LOOP_STEP, LOOPS, LAST_STEP = -3, 2, 5, 17


def steps(eng, step, query_group):
    for g in range(NG):
        query_group(g)
        if g < 2:
            step(Batch(FIRST_STEP + g))
    for s in range(FIRST_STEP + 2, LOOP_STEP):
        step(Batch(s))
    with eng.Fori(0, LOOPS) as i:
        for s in range(LOOP_STEP, LOOP_STEP + 2):
            step(Batch(s, i))
    for s in range(LOOP_STEP + 2 * LOOPS, LAST_STEP + 1):
        step(Batch(s))


def need(eng, sem, value):
    if isinstance(value, int) and value <= 0:
        return
    eng.wait_ge(sem, value)


def build(nc, x, ctx_t, wq, wk, wv, wo, bo, gw1, small, gb2, w1, eb, w2, out):
    with ExitStack() as stack:
        def psum(name, shape, dt=F32):
            return stack.enter_context(nc.psum_tensor(name, shape, dt))

        def sem(name):
            return stack.enter_context(nc.semaphore(name))

        def size(shape, dt):
            n = 2 if dt == BF16 else 4
            for d in shape[1:]:
                n *= d
            return n

        class Region:

            def __init__(self, start, end):
                self.at, self.end = start, end

            def take(self, name, shape, dt):
                t = nc.alloc_sbuf_tensor_at(name, shape, dt, offset=self.at)
                self.at += (size(shape, dt) + 31) // 32 * 32
                assert self.at <= self.end, (name, self.at, self.end)
                return t

        start = (nc.sbuf_base + 31) // 32 * 32
        RAW = 2 * IT * 512 * 4
        W1B = 2 * 2 * IT * 512 * 4
        XTB = 2 * IT * T * 4
        W2B = 2 * 2 * OT * 512 * 4
        at_w2 = start + RAW
        at_w1 = at_w2 + W2B - XTB - W1B
        at_xt = at_w1 + W1B
        at_main = at_xt + XTB

        w_raw = nc.alloc_sbuf_tensor_at("w_raw", [P, 2, IT, 512], F32, offset=start)
        w1_parts = nc.alloc_sbuf_tensor_at("w1_parts", [P, 2, 2, IT, 512], F32R, offset=at_w1)
        xt_parts = nc.alloc_sbuf_tensor_at("xt_parts", [P, 2, IT, T], F32R, offset=at_xt)
        w2_parts = nc.alloc_sbuf_tensor_at("w2_parts", [P, 2, OT // 2, 2, 2, 512], F32R, offset=at_w2)

        ffn = Region(at_main, nc.sbuf_usable_end)
        gates = ffn.take("gates", [P, PAT, C + E], F32)
        y = ffn.take("y", [P, TT, C], F32)
        at_acc = ffn.at
        acc = ffn.take("acc", [P, TT, DFF], F32)
        h_high = nc.alloc_sbuf_tensor_at("h_high", [P, TT, OT, P], F32R, offset=at_acc)
        h_low = ffn.take("h_low", [P, TT, OT, P], F32R)
        keep = Region(ffn.at, nc.sbuf_usable_end)
        ident = keep.take("ident", [P, P], F32)
        ident_b = keep.take("ident_b", [P, P], BF16)
        ident_e = keep.take("ident_e", [E, E], F32)
        small_sb = keep.take("small_sb", [P, 8 + 2 * E], F32)
        bq_sb, bk_sb, bv_sb, gb1_sb = (small_sb[:, 2 * n:2 * n + 2] for n in range(4))
        gw2_sb = small_sb[:, 8:8 + 2 * E].rearrange("p (k e) -> p k e", k=2)
        gb2_sb = keep.take("gb2_sb", [E, 1], F32)
        gate_t = keep.take("gate_t", [E, NQ], F32)
        max_rows = keep.take("max_rows", [D, 2, NQ], BF16)
        stats = keep.take("stats", [NQ, GB, 6], F32)
        mean_var = keep.take("mean_var", [NQ, GB, 2], F32)
        half_var = keep.take("half_var", [NQ, GB], F32)
        magic = keep.take("magic", [NQ, GB], I32)
        one_half = keep.take("one_half", [NQ, GB], F32)
        half_bits = keep.take("half_bits", [NQ, GB], I32)
        root_tmp = keep.take("root_tmp", [NQ, GB], F32)
        rstd = keep.take("rstd", [NQ, GB], F32)
        maxima = keep.take("maxima", [NQ, 2, H], F32)
        max_parts = keep.take("max_parts", [NQ, 2, 2, HH], BF16)
        recip = keep.take("recip", [NQ, H], F32)

        front = Region(at_w2, at_w1)
        k_f32 = front.take("k_f32", [P, 2, KVE], F32)
        k_rest = front.take("k_rest", [P, 2, KVE], F32)
        k_parts = front.take("k_parts", [P, 3, 2, KVP], BF16)
        o_full = front.take("o_full", [P, 4 * NQ], F32)
        o_norm = front.take("o_norm", [NQ, H, D], F32)
        ot_high = front.take("ot_high", [P, 2, NQ], F32R)
        ot_low = front.take("ot_low", [P, 2, NQ], F32R)
        x_norm = front.take("x_norm", [NQ, C], F32)
        x_bias = front.take("x_bias", [NQ, C], F32)
        x_mid = front.take("x_mid", [NQ, 2, C], F32)

        main = Region(at_main, ffn.at)
        w_f32 = main.take("w_f32", [P, 5, IT, C], F32)
        w_high = main.take("w_high", [P, 5, IT, C], F32R)
        w_low = main.take("w_low", [P, 5, IT, C], F32R)
        x_all = main.take("x_all", [NQ, B, C], F32)
        probs = main.take("probs", [P, 4, CH, HQ * NQ], F32)
        v_ones = main.take("v_ones", [P, 2, CH, H, VW], F32)
        q_stack = main.take("q_stack", [P, 2, H * NQ], BF16)
        k_stack = main.take("k_stack", [P, 2, H, KVP], BF16)
        at_ctx = main.at
        c_raw = main.take("c_raw", [P, 2, IT, KVE], F32)
        c_high = main.take("c_high", [P, 2, IT, KVE], F32R)
        c_low = main.take("c_low", [P, 2, IT, KVE], F32R)
        bias_row = main.take("bias_row", [NQ, C], F32)
        bo_row = main.take("bo_row", [NQ, C], F32)
        bv_wide = main.take("bv_wide", [P, 2, NQ], F32)
        gate = Region(at_ctx, main.at)
        g_relu = gate.take("g_relu", [P, 2, GW], F32)
        h_sums = gate.take("h_sums", [P, 2, NG, NQ], F32)
        h_sum = gate.take("h_sum", [P, 2, NQ], F32)
        eb_sb = gate.take("eb_sb", [E, GCOLS], F32)
        g_row = gate.take("g_row", [NQ, GCOLS], F32)
        pre = Region(at_w1, at_main)
        xq = pre.take("xq", [NQ, 2, GB, C], F32)
        xqt_high = pre.take("xqt_high", [P, 2, IT, GW], F32R)
        xqt_low = pre.take("xqt_low", [P, 2, IT, GW], F32R)
        q_f32 = pre.take("q_f32", [P, 2, GB, 2, NQ], F32)
        q_parts = pre.take("q_parts", [P, 2, 3, GB, 2, NQ], BF16)
        q_rest = pre.take("q_rest", [P, GB, 2, NQ], F32)
        minus_ones = pre.take("minus_ones", [P, 2 * 2 * H * KVP // P], BF16)

        WQ, WK, WV, WO, GW1 = range(5)

        k_dram = nc.dram_tensor("k_dram", [2, 3, D, H * KVP], BF16, kind="Internal").ap()
        q_dram = nc.dram_tensor("q_dram", [B, 3, D, H * NQ], BF16, kind="Internal").ap()
        xmid_dram = nc.dram_tensor("xmid_dram", [T, C], F32, kind="Internal").ap()
        gate_dram = nc.dram_tensor("gate_dram", [2 * NQ, GCOLS], F32, kind="Internal").ap()

        banks = psum("banks", [P, 8, 512])
        ps_max = [banks[:, 0:2, :], banks[:, 2:4, :]]
        ps_max_t = banks[0:D, 2, 384:448].bitcast(BF16)[:, 0:NQ]
        ps_sc = banks[:, 4:6, :]
        ps_qt = [banks[:, 0:2, :], banks[:, 2:4, :]]
        ps_q = banks[:, 4:6, :]
        ps_o = banks[:, 6, :]
        ps_w = banks[:, 7, :]

        x_loaded = [sem(f"x_loaded{g}") for g in range(NG)]
        w_loaded = [sem(f"w_loaded{n}") for n in range(5)]
        small_loaded = sem("small_loaded")
        ones_set, zero_set, ident_set = sem("ones_set"), sem("zero_set"), sem("ident_set")
        minus_set = sem("minus_set")
        stack_set, pad_set = sem("stack_set"), sem("pad_set")
        w_high_done = sem("w_high_done")
        w_low_done = [sem(f"w_low_done{n}") for n in range(5)]
        bv_wide_done, bias_mm, bias_done = sem("bv_wide_done"), sem("bias_mm"), sem("bias_done")
        q_stat, q_aggr, q_norm = sem("q_stat"), sem("q_aggr"), sem("q_norm")
        root_set, eps_added, bits_halved, root_done = sem("root_set"), sem("eps_added"), sem("bits_halved"), sem("root_done")
        q_tr, q_xhigh, q_xlow, q_mm = sem("q_tr"), sem("q_xhigh"), sem("q_xlow"), sem("q_mm")
        q_evac, qr_done, q2_done, q3_done = sem("q_evac"), sem("qr_done"), sem("q2_done"), sem("q3_done")
        q_stored = [sem(f"q_stored{g}") for g in range(NG)]
        c_loaded = [sem("c_loaded0"), sem("c_loaded1")]
        c_high_done, c_low_done = sem("c_high_done"), sem("c_low_done")
        k_mm, v_mm, k_evac, v_evac = sem("k_mm"), sem("v_mm"), sem("k_evac"), sem("v_evac")
        kr_done, k2_done, k3_done = sem("kr_done"), sem("k2_done"), sem("k3_done")
        k_stored = sem("k_stored")
        stack_loaded = [[sem(f"stack_loaded{s}{h}") for h in range(2)] for s in range(2)]
        max_mm, max_red, m1_done, m2_done = sem("max_mm"), sem("max_red"), sem("m1_done"), sem("m2_done")
        max_tr, max_copied = sem("max_tr"), sem("max_copied")
        max_loaded = [sem("max_loaded0"), sem("max_loaded1")]
        sc_mm, exp_done, pv_mm = sem("sc_mm"), sem("exp_done"), sem("pv_mm")
        o_copied, o_tr, recip_done, o_normed = sem("o_copied"), sem("o_tr"), sem("recip_done"), sem("o_normed")
        ot_mm, ot_high_done, ot_low_done, out_mm = (
            sem("ot_mm"), sem("ot_high_done"), sem("ot_low_done"), sem("out_mm"))
        xb_done, xmid_done, stat_done, aggr_done = (
            sem("xb_done"), sem("xmid_done"), sem("stat_done"), sem("aggr_done"))
        xn_done, xt_mm, xt_high_done, xt_low_done = (
            sem("xn_done"), sem("xt_mm"), sem("xt_high_done"), sem("xt_low_done"))
        xmid_stored = [sem("xmid_stored0"), sem("xmid_stored1")]
        eb_loaded, g_mm, g_relu_done, g_part = sem("eb_loaded"), sem("g_mm"), sem("g_relu_done"), sem("g_part")
        g_sum, g_gate_mm, g_t_done, g_exp_mm = sem("g_sum"), sem("g_gate_mm"), sem("g_t_done"), sem("g_exp_mm")
        g_row_done, g_stored, gates_loaded = sem("g_row_done"), sem("g_stored"), sem("gates_loaded")
        acc_loaded = [sem(f"acc_loaded{t}") for t in range(TT)]
        y_loaded, y_ready = sem("y_loaded"), sem("y_ready")
        raw_loaded = [sem("raw_loaded0"), sem("raw_loaded1")]
        wh_done, wl_done = sem("wh_done"), sem("wl_done")
        z1_mm, acc_done = sem("z1_mm"), sem("acc_done")
        h_tr, h_high_done, h_low_done = sem("h_tr"), sem("h_high_done"), sem("h_low_done")
        z2_mm, y_done, out_stored = sem("z2_mm"), sem("y_done"), sem("out_stored")

        def three(pe, out_ap, left, right, tiles, stop_last=True):
            n = 0
            for a, b in ((0, 0), (0, 1), (1, 0)):
                for k in range(tiles):
                    last = pe.matmul(out_ap, left(a, k), right(b, k), start=(n == 0), stop=(n == 3 * tiles - 1))
                    n += 1
            return last

        L1N = 2 * E
        L2P = E // 2
        L2C = OT // 2
        NB1 = 7

        block = stack.enter_context(nc.Block())

        @block.sync
        def _(sp):
            def load_x(g):
                sp.dma_start(x_all[:, GB * g:GB * g + GB, :],
                             x[GB * g:GB * g + GB].rearrange("b q c -> q b c")).then_inc(x_loaded[g], 16)

            def load_w(n, w):
                sp.dma_start(w_f32[:, n], w).then_inc(w_loaded[n], 16)

            load_x(0)
            load_w(WQ, wq)
            sp.dma_start(small_sb[:], small).then_inc(small_loaded, 16)
            load_x(1)
            load_w(WK, wk)
            def load_context(b):
                if not b.exists:
                    return
                need(sp, c_high_done, b.times(1, -1))
                need(sp, c_low_done, b.times(1, -1))
                dram = ctx_t[:, b.times(1), :, :] if b.i is None else ctx_t[:, bass.ds(b.times(1), 1), :, :]
                sp.dma_start(c_raw[:, b.slot, :, 0:NKV], dram).then_inc(c_loaded[b.slot], 16)

            sp.wait_ge(pad_set, 1)
            load_context(Batch(0))
            load_x(2)
            load_x(3)
            load_w(WV, wv)
            sp.wait_ge(minus_set, 1)
            sp.dma_start(k_stack[QROWS:SROWS].rearrange("p s h t -> p (s h t)"), minus_ones[:]).then_inc(stack_set, 16)
            load_w(WO, wo)
            sp.dma_start(bo_row[:], bo.to_broadcast([NQ, C])).then_inc(small_loaded, 16)
            sp.dma_start(gb2_sb[:], gb2).then_inc(small_loaded, 16)
            load_w(GW1, gw1)
            for n in range(2):
                sp.dma_start(w_raw[:, n], w1[n]).then_inc(raw_loaded[n], 16)

            def load_queries(b, h):
                if b.i is None and b.c < NG:
                    sp.wait_ge(q_stored[b.c], 16 * GB)
                need(sp, sc_mm, b.times(12, -24 + 6 * (h + 1)))
                cols = slice(h * HH * NQ, (h + 1) * HH * NQ)
                q = q_dram[b.times(1)] if b.i is None else q_dram[bass.ds(b.times(1), 1)].rearrange("a p d t -> (a p) d t")
                for row, part, reps in ((0, 0, 3), (3 * D, 1, 2), (5 * D, 2, 1)):
                    src = q[part:part + 1, :, cols].to_broadcast([reps, D, HH * NQ])
                    sp.dma_start(q_stack[row:row + reps * D, b.slot, cols], src).then_inc(stack_loaded[b.slot][h], 16)

            def load_keys(b, h):
                need(sp, k_stored, b.times(16, 16))
                need(sp, sc_mm, b.times(12, -24 + 6 * (h + 1)))
                k = k_dram[b.slot]
                for row, parts in ((0, 3), (3 * D, 2), (5 * D, 1)):
                    sp.dma_start(
                        k_stack[row:row + parts * D, b.slot, h * HH:(h + 1) * HH, :].rearrange("p h t -> p (h t)"),
                        k[0:parts, :, h * HH * KVP:(h + 1) * HH * KVP].rearrange("p d t -> (p d) t"),
                    ).then_inc(stack_loaded[b.slot][h], 16)

            def load_maxima(b, h):
                need(sp, max_copied, b.times(2, h + 1))
                sp.dma_start(q_stack[QROWS:SROWS, b.slot, h * HH * NQ:(h + 1) * HH * NQ],
                             max_rows[:, h, :]).then_inc(max_loaded[h], 16)

            def step(s):
                if (s + -2).exists:
                    b = s + -2
                    need(sp, xmid_done, b.times(1, 1))
                    dst = xmid_dram.rearrange("(b q) c -> b q c", q=NQ)
                    dst = dst[b.times(1)] if b.i is None else dst[bass.ds(b.times(1), 1)].rearrange("a q c -> (a q) c")
                    sp.dma_start(dst, x_mid[:, b.slot, :]).then_inc(xmid_stored[b.slot], 16)
                b = s + 1
                if b.exists:
                    load_queries(b, 1)
                    load_keys(b, 1)
                if s.exists:
                    load_maxima(s, 1)
                load_context(s + 4)
                b = s + 2
                if b.exists:
                    for h in range(2):
                        need(sp, stack_loaded[b.slot][h], b.uses(96) + -96)
                    need(sp, k3_done, b.times(1, 1))
                    sp.dma_start(k_dram[b.slot].rearrange("p d (h t) -> (d h) p t", h=HH),
                                 k_parts[:].rearrange("p k m t -> p k (m t)")).then_inc(k_stored, 16)
                    load_queries(b, 0)
                if (s + 1).exists:
                    load_maxima(s + 1, 0)
                if b.exists:
                    load_keys(b, 0)

            steps(sp, step, lambda g: None)

            sp.wait_ge(c_low_done, B)
            sp.wait_ge(v_mm, CH * B)
            sp.wait_ge(ident_set, 3)
            sp.dma_start(eb_sb[:, 0:DFF + C], eb).then_inc(eb_loaded, 16)
            sp.dma_start(eb_sb[:, DFF + C:GCOLS], ident_e[:]).then_inc(eb_loaded, 16)

            def load_raw(freed, slot, src):
                sp.wait_ge(wl_done, freed)
                sp.dma_start(w_raw[:, slot], src).then_inc(raw_loaded[slot], 16)

            for n in range(2):
                load_raw(n + 1, n, w1[2 + n])

            sp.wait_ge(g_row_done, 3)
            for n in range(2):
                sp.dma_start(gate_dram[n * NQ:(n + 1) * NQ], g_row[:]).then_inc(g_stored, 16)
            sp.wait_ge(g_stored, 32)

            def gate_rows(t):
                p = t % PAT
                return gate_dram[16 * p:16 * p + P]

            sp.dma_start(acc[:, 0, :], gate_rows(0)[:, 0:DFF]).then_inc(acc_loaded[0], 16)
            for p in range(PAT):
                sp.dma_start(gates[:, p, :], gate_rows(p)[:, DFF:GCOLS]).then_inc(gates_loaded, 16)
            for t in range(1, TT):
                sp.dma_start(acc[:, t, :], gate_rows(t)[:, 0:DFF]).then_inc(acc_loaded[t], 16)
            for s in range(2):
                sp.wait_ge(xmid_stored[s], 16 * B // 2)
            sp.dma_start(y[:], xmid_dram.rearrange("(t p) c -> p t c", p=P)).then_inc(y_loaded, 16)

            with sp.Fori(2, E) as e:
                for n in range(2):
                    load_raw(e * 2 + (n - 1), n, w1[bass.ds(e * 2 + n, 1)].rearrange("a p k n -> (a p) k n"))
            with sp.Fori(0, L2P) as ep:
                for c in range(L2C):
                    load_raw(ep * L2C + (L1N + c - 1), c % 2,
                             w2[bass.ds(ep * L2C + c, 1)].rearrange("a p k n -> (a p) k n"))

            outs = out.rearrange("(t p) c -> t p c", p=P)
            for t in range(TT):
                sp.wait_ge(y_done, 2 * (TT * (L2P - 1) + t + 1))
                sp.dma_start(outs[t], y[:, t, :]).then_inc(out_stored, 16)
            sp.wait_ge(out_stored, 16 * TT)

        @block.gpsimd
        def _(pool):
            pool.memset(c_raw[:, :, :, NKV:KVE], 0.0).then_inc(pad_set, 1)
            pool.memset(ident[:], 0.0).then_inc(zero_set, 1)
            pool.memset(ident_b[:], 0.0).then_inc(zero_set, 1)
            pool.memset(ident_e[:], 0.0).then_inc(zero_set, 1)
            pool.wait_ge(zero_set, 3)
            for m, n in ((ident, P), (ident_b, P), (ident_e, E)):
                pool.affine_select(out=m[:], in_=m[:], compare_op=ALU.not_equal, fill=1.0, base=0,
                                   pattern=[[-1, n]], channel_multiplier=1).then_inc(ident_set, 1)
            pool.memset(magic[:], MAGIC)
            pool.memset(one_half[:], 1.5).then_inc(root_set, 1)
            pool.wait_ge(root_set, 1)
            pool.memset(minus_ones[:], -1.0).then_inc(minus_set, 1)
            pool.memset(k_parts[:, :, :, KVE:KVP], 0.0).then_inc(ones_set, 1)
            pool.memset(v_ones[:, :, :, :, D:VW], 1.0).then_inc(ones_set, 1)

            def inverse_root(n, before):
                y, t = rstd[:, 0:n], root_tmp[:, 0:n]
                pool.tensor_tensor(y.bitcast(I32), magic[:, 0:n], half_bits[:, 0:n], ALU.subtract).then_inc(root_done, 1)
                for k in range(ROOT_STEPS):
                    pool.wait_ge(root_done, before + (4 * k + 1))
                    pool.tensor_tensor(t, y, y, ALU.mult).then_inc(root_done, 1)
                    pool.wait_ge(root_done, before + (4 * k + 2))
                    pool.tensor_tensor(t, t, half_var[:, 0:n], ALU.mult).then_inc(root_done, 1)
                    pool.wait_ge(root_done, before + (4 * k + 3))
                    pool.tensor_tensor(t, one_half[:, 0:n], t, ALU.subtract).then_inc(root_done, 1)
                    pool.wait_ge(root_done, before + (4 * k + 4))
                    pool.tensor_tensor(y, y, t, ALU.mult).then_inc(root_done, 1)

            def query_root(g):
                pool.wait_ge(bits_halved, g + 1)
                need(pool, q_norm, GB * g)
                inverse_root(GB, ROOT_OPS * g)

            def weight_low(n):
                pool.wait_ge(w_high_done, n + 1)
                pool.tensor_tensor(w_low[:, n], w_f32[:, n], w_high[:, n], ALU.subtract).then_inc(w_low_done[n], 1)

            def query_group(g):
                if g == 0:
                    query_root(0)
                if g + 1 < NG:
                    query_root(g + 1)
                pool.wait_ge(q_evac, 2 * (g + 1))
                need(pool, q3_done, g)
                pool.tensor_tensor(q_rest[:], q_f32[:, g % 2], q_parts[:, g % 2, 0], ALU.subtract).then_inc(qr_done, 1)
                if g == 0:
                    weight_low(WK)
                    weight_low(WV)

            def step(s):
                b = s + 2
                if b.exists:
                    need(pool, k_evac, b.times(2, 2))
                    pool.tensor_tensor(k_rest[:], k_f32[:], k_parts[:, 0, :, 0:KVE], ALU.subtract)\
                        .then_inc(kr_done, 1)
                    need(pool, k2_done, b.times(1, 1))
                    pool.tensor_tensor(k_parts[:, 2, :, 0:KVE], k_rest[:], k_parts[:, 1, :, 0:KVE], ALU.subtract)\
                        .then_inc(k3_done, 1)
                b = s + -1
                if b.exists:
                    if b.i is None and b.c == 0:
                        pool.wait_ge(bias_done, 1)
                    need(pool, xmid_done, b.times(1, 0))
                    src = x_all[:, b.times(1), :] if b.i is None else x_all[:, bass.ds(b.times(1), 1), :]
                    pool.tensor_tensor(x_bias[:], src, bias_row[:], ALU.add).then_inc(xb_done, 1)
                b = s + 3
                if b.exists:
                    need(pool, c_high_done, b.times(1, 1))
                    pool.tensor_tensor(c_low[:, b.slot], c_raw[:, b.slot], c_high[:, b.slot], ALU.subtract)\
                        .then_inc(c_low_done, 1)
                b = s + -1
                if b.exists:
                    need(pool, bits_halved, b.times(1, 1) + NG)
                    inverse_root(1, b.times(ROOT_OPS) + ROOT_OPS * NG)

            steps(pool, step, query_group)

            def low_part(r, slot, dst):
                pool.wait_ge(wh_done, r)
                pool.tensor_tensor(dst(1), w_raw[:, slot], dst(0), ALU.subtract).then_inc(wl_done, 1)

            for s in range(2):
                low_part(s + 1, s, lambda part: w1_parts[:, s, part])
            pool.wait_ge(y_loaded, 16)
            pool.wait_ge(gates_loaded, 16 * PAT)
            for n in range(TT // PAT):
                rows = slice(n * PAT, (n + 1) * PAT)
                pool.tensor_tensor(y[:, rows, :], y[:, rows, :], gates[:, :, 0:C], ALU.add).then_inc(y_ready, 1)
            with pool.Fori(1, E) as e:
                for s in range(2):
                    low_part(e * 2 + s + 1, s, lambda part: w1_parts[:, s, part])
            with pool.Fori(0, L2P) as ep:
                for c in range(L2C):
                    low_part(ep * L2C + (L1N + c + 1), c % 2,
                             lambda part: w2_parts[:, bass.ds(ep % 2, 1), c, part].rearrange("p s a n -> p (s a) n"))

        @block.scalar
        def _(act):
            def weight_high(n):
                act.wait_ge(w_loaded[n], 16)
                act.activation(w_high[:, n], w_f32[:, n], ACT.Copy).then_inc(w_high_done, 1)

            def query_store(g):
                act.wait_ge(q3_done, g + 1)
                for j in range(GB):
                    act.dma_start(q_dram[GB * g + j].rearrange("p d (h t) -> (d h) p t", h=HH),
                                  q_parts[:, g % 2, :, j].rearrange("p k m t -> p k (m t)")).then_inc(q_stored[g], 16)

            def query_high(g):
                act.wait_ge(q_tr, g + 1)
                need(act, q_mm, 2 * (g - 1))
                act.activation(xqt_high[:, g % 2], ps_qt[g % 2][:, :, 0:GW], ACT.Copy).then_inc(q_xhigh, 1)

            def query_group(g):
                if g == 0:
                    weight_high(WQ)
                    query_high(0)
                    weight_high(WK)
                    weight_high(WV)
                    act.wait_ge(small_loaded, 16)
                need(act, qr_done, g - 1)
                if g >= 2:
                    act.wait_ge(q_stored[g - 2], 16 * GB)
                for m in range(2):
                    act.wait_ge(q_mm, 2 * g + m + 1)
                    ps = ps_q[:, m, 0:GW].rearrange("p (b t) -> p b t", b=GB)
                    act.activation(q_f32[:, g % 2, :, m, :], ps, ACT.Identity, bias=bq_sb[:, m:m + 1])
                    act.activation(q_parts[:, g % 2, 0, :, m, :], ps, ACT.Identity, bias=bq_sb[:, m:m + 1])\
                        .then_inc(q_evac, 1)
                if g + 1 < NG:
                    query_high(g + 1)
                query_store(g)
                if g == NG - 1:
                    weight_high(WO)
                    weight_high(GW1)

            def exp(b, u):
                if not b.exists:
                    return
                need(act, sc_mm, b.times(12, u + 1))
                need(act, pv_mm, b.times(4, -4 + u // CH + 1))
                act.activation(probs[:, u // CH, u % CH], ps_sc[:, u % 2, 0:HQ * NQ], ACT.Exp,
                               scale=SCALE).then_inc(exp_done, 1)

            def key_evac(b, m):
                if b.exists:
                    need(act, k_mm, b.times(2, m + 1))
                    need(act, kr_done, b.times(1, 0))
                    need(act, k_stored, b.times(16))
                    act.activation(k_f32[:, m, :], ps_w[:, 0:KVE], ACT.Identity, bias=bk_sb[:, m:m + 1])
                    act.activation(k_parts[:, 0, m, 0:KVE], ps_w[:, 0:KVE], ACT.Identity, bias=bk_sb[:, m:m + 1])\
                        .then_inc(k_evac, 1)

            def value_evac(b, c):
                if b.exists:
                    n = CHROWS[c]
                    need(act, v_mm, b.times(3, c + 1))
                    need(act, pv_mm, b.times(4, -4))
                    act.activation(v_ones[0:n, b.slot, c, :, 0:D],
                                   ps_w[0:n, 0:C].rearrange("p (h d) -> p h d", h=H), ACT.Copy).then_inc(v_evac, 1)

            def max_copy(b, h):
                if b.exists:
                    need(act, max_tr, b.times(2, h + 1))
                    need(act, max_loaded[h], b.times(16))
                    act.activation(max_rows[:, h, :], ps_max_t, ACT.Copy).then_inc(max_copied, 1)

            def step(s):
                old, last, nxt, new = s + -2, s + -1, s + 1, s + 3
                exp(s, 0)
                max_copy(s, 1)
                value_evac(nxt, 0)
                if last.exists:
                    need(act, pv_mm, last.times(4, 4))
                    need(act, o_tr, last.times(1))
                    act.activation(o_full[:], ps_o[:, 0:4 * NQ], ACT.Copy).then_inc(o_copied, 1)
                exp(s, 1)
                if old.exists:
                    need(act, xt_mm, old.times(1, 1))
                    at = old.times(NQ)
                    dst = xt_parts[:, 0, :, at:at + NQ] if old.i is None else xt_parts[:, 0, :, bass.ds(at, NQ)]
                    act.activation(dst, ps_w[:, 0:2 * NQ].rearrange("p (a t) -> p a t", a=2), ACT.Copy)\
                        .then_inc(xt_high_done, 1)
                exp(s, 2)
                exp(s, 3)
                value_evac(nxt, 1)
                exp(s, 4)
                value_evac(nxt, 2)
                exp(s, 5)
                if new.exists:
                    need(act, c_loaded[new.slot], new.uses(16))
                    need(act, v_mm, new.times(3, -3))
                    act.activation(c_high[:, new.slot], c_raw[:, new.slot], ACT.Copy).then_inc(c_high_done, 1)
                if last.exists:
                    need(act, ot_mm, last.times(1, 1))
                    act.activation(ot_high[:], ps_w[:, 0:2 * NQ].rearrange("p (a t) -> p a t", a=2), ACT.Copy)\
                        .then_inc(ot_high_done, 1)
                exp(s, 6)
                max_copy(nxt, 0)
                exp(s, 7)
                exp(s, 8)
                key_evac(new, 0)
                exp(s, 9)
                exp(s, 10)
                exp(s, 11)
                key_evac(new, 1)

            act.wait_ge(pad_set, 1)
            steps(act, step, query_group)

            def high_part(loaded, slot, dst):
                act.wait_ge(raw_loaded[slot], loaded)
                act.activation(dst, w_raw[:, slot], ACT.Copy).then_inc(wh_done, 1)

            for s in range(2):
                high_part(16, s, w1_parts[:, s, 0])

            for g in range(NG):
                for m in range(2):
                    n = 2 * g + m
                    act.wait_ge(g_mm, n + 1)
                    need(act, g_part, n - 1)
                    act.activation(g_relu[:, m, :], banks[:, m, 0:GW], ACT.Relu, bias=gb1_sb[:, m:m + 1])\
                        .then_inc(g_relu_done, 1)
            act.wait_ge(g_gate_mm, 1)
            act.activation(gate_t[:], banks[0:E, 2, 0:NQ], ACT.Identity, bias=gb2_sb[:, 0:1], scale=1.0 / B)\
                .then_inc(g_t_done, 1)
            for n in range(3):
                cols = slice(512 * n, min(512 * (n + 1), GCOLS))
                act.wait_ge(g_exp_mm, n + 1)
                act.activation(g_row[:, cols], banks[0:NQ, 3 + n, 0:cols.stop - cols.start], ACT.Copy)\
                    .then_inc(g_row_done, 1)

            with act.Fori(1, E) as e:
                for s in range(2):
                    act.wait_ge(z1_mm, e * (2 * TT) + (s - 1) * TT)
                    high_part(e * 16 + 16, s, w1_parts[:, s, 0])
            for c in range(L2C):
                if c >= 2:
                    act.wait_ge(z1_mm, TT * (L1N - 3 + c))
                high_part(16 * (E + c // 2 + 1), c % 2, w2_parts[:, 0, c, 0])
            for t in range(TT):
                act.wait_ge(h_tr, t + 1)
                act.activation(h_high[:, t], banks[:, 4 + 2 * (t % 2):6 + 2 * (t % 2), :], ACT.Relu)\
                    .then_inc(h_high_done, 1)
                if t == 1:
                    for c in range(L2C):
                        high_part(16 * (E + 2 + c // 2 + 1), c % 2, w2_parts[:, 1, c, 0])
            with act.Fori(2, L2P) as ep:
                act.wait_ge(z2_mm, ep * TT - TT)
                for c in range(L2C):
                    high_part(ep * 32 + 16 * (E + c // 2 + 1), c % 2,
                              w2_parts[:, bass.ds(ep % 2, 1), c, 0].rearrange("p s a n -> p (s a) n"))

        @block.vector
        def _(dve):
            def halve_bits(n, aggregated, count):
                value, of = aggregated
                dve.wait_ge(of, value)
                dve.tensor_scalar(half_var[:, 0:n], mean_var[:, 0:n, 1], EPS, 0.5, ALU.add, ALU.mult)\
                    .then_inc(eps_added, 1)
                dve.wait_ge(eps_added, count)
                dve.tensor_scalar(half_bits[:, 0:n], half_var[:, 0:n].bitcast(I32), 1, None,
                                  ALU.logical_shift_right).then_inc(bits_halved, 1)

            def query_stats(g):
                dve.wait_ge(x_loaded[g], 16)
                need(dve, root_done, ROOT_OPS * g)
                for j in range(GB):
                    dve.bn_stats(stats[:, j, :], x_all[:, GB * g + j, :]).then_inc(q_stat, 1)
                for j in range(GB):
                    dve.wait_ge(q_stat, GB * g + j + 1)
                    dve.bn_aggr(mean_var[:, j, :], stats[:, j, :]).then_inc(q_aggr, 1)
                halve_bits(GB, (GB * (g + 1), q_aggr), g + 1)

            def query_norm(g):
                dve.wait_ge(root_done, ROOT_OPS * (g + 1))
                need(dve, q_tr, g - 1)
                for j in range(GB):
                    dve.tensor_scalar(xq[:, g % 2, j, :], x_all[:, GB * g + j, :], mean_var[:, j, 0:1],
                                      rstd[:, j:j + 1], ALU.subtract, ALU.mult).then_inc(q_norm, 1)

            def query_group(g):
                if g == 0:
                    query_stats(0)
                    dve.wait_ge(w_high_done, WQ + 1)
                    dve.tensor_tensor(w_low[:, WQ], w_f32[:, WQ], w_high[:, WQ], ALU.subtract)\
                        .then_inc(w_low_done[WQ], 1)
                    query_norm(0)
                if g + 1 < NG:
                    query_stats(g + 1)
                dve.wait_ge(q_xhigh, g + 1)
                need(dve, q_mm, 2 * (g - 1))
                dve.tensor_tensor(xqt_low[:, g % 2], ps_qt[g % 2][:, :, 0:GW], xqt_high[:, g % 2], ALU.subtract)\
                    .then_inc(q_xlow, 1)
                if g + 1 < NG:
                    query_norm(g + 1)
                dve.wait_ge(qr_done, g + 1)
                if g >= 2:
                    dve.wait_ge(q_stored[g - 2], 16 * GB)
                dve.tensor_copy(q_parts[:, g % 2, 1], q_rest[:]).then_inc(q2_done, 1)
                dve.wait_ge(q2_done, g + 1)
                dve.tensor_tensor(q_parts[:, g % 2, 2], q_rest[:], q_parts[:, g % 2, 1], ALU.subtract)\
                    .then_inc(q3_done, 1)
                if g == NG - 1:
                    dve.wait_ge(small_loaded, 16 * 3)
                    dve.tensor_copy(bv_wide[:], bv_sb.unsqueeze(2).to_broadcast([P, 2, NQ])).then_inc(bv_wide_done, 1)
                    for n in (WO, GW1):
                        dve.wait_ge(w_high_done, n + 1)
                        dve.tensor_tensor(w_low[:, n], w_f32[:, n], w_high[:, n], ALU.subtract)\
                            .then_inc(w_low_done[n], 1)
                    dve.wait_ge(bias_mm, 1)
                    dve.tensor_tensor(bias_row[:], ps_o[0:NQ, 0:C], bo_row[:], ALU.add).then_inc(bias_done, 1)

            def reduce_max(b, k):
                if b.exists:
                    need(dve, max_mm, b.times(8, k + 1))
                    dve.tensor_reduce(maxima[:, b.slot, 2 * k:2 * k + 2], ps_max[k % 2][0:NQ, :, 0:NKV], AX_X, ALU.max)\
                        .then_inc(max_red, 1)

            def max_first(b, h):
                if b.exists:
                    need(dve, max_red, b.times(8, 4 * h + 4))
                    need(dve, max_tr, b.times(2, h - 1))
                    dve.tensor_copy(max_parts[:, h, 0, :], maxima[:, b.slot, HH * h:HH * h + HH]).then_inc(m1_done, 1)

            def max_second(b, h):
                if b.exists:
                    need(dve, m1_done, b.times(2, h + 1))
                    dve.tensor_tensor(max_parts[:, h, 1, :], maxima[:, b.slot, HH * h:HH * h + HH],
                                      max_parts[:, h, 0, :], ALU.subtract).then_inc(m2_done, 1)

            def step(s):
                old, last, nxt, new = s + -2, s + -1, s + 1, s + 2
                max_first(s, 1)
                max_second(s, 1)
                if old.exists:
                    need(dve, root_done, old.times(ROOT_OPS, ROOT_OPS) + ROOT_OPS * NG)
                    dve.tensor_scalar(x_norm[:], x_mid[:, old.slot, :], mean_var[:, 0, 0:1], rstd[:, 0:1],
                                      ALU.subtract, ALU.mult).then_inc(xn_done, 1)
                reduce_max(nxt, 0)
                if old.exists:
                    need(dve, xt_high_done, old.times(1, 1))
                    at = old.times(NQ)
                    cols = slice(at, at + NQ) if old.i is None else bass.ds(at, NQ)
                    dve.tensor_tensor(xt_parts[:, 1, :, cols], ps_w[:, 0:2 * NQ].rearrange("p (a t) -> p a t", a=2),
                                      xt_parts[:, 0, :, cols], ALU.subtract).then_inc(xt_low_done, 1)
                reduce_max(nxt, 1)
                if last.exists:
                    need(dve, o_tr, last.times(1, 1))
                    sums = ps_o[0:NQ, :].rearrange("p (h w) -> p h w", w=VW)
                    dve.reciprocal(recip[:], sums[:, :, D]).then_inc(recip_done, 1)
                    need(dve, recip_done, last.times(1, 1))
                    dve.tensor_tensor(o_norm[:], sums[:, :, 0:D], recip[:].unsqueeze(2).to_broadcast([NQ, H, D]),
                                      ALU.mult).then_inc(o_normed, 1)
                if new.exists:
                    need(dve, kr_done, new.times(1, 1))
                    dve.tensor_copy(k_parts[:, 1, :, 0:KVE], k_rest[:]).then_inc(k2_done, 1)
                reduce_max(nxt, 2)
                reduce_max(nxt, 3)
                max_first(nxt, 0)
                max_second(nxt, 0)
                reduce_max(nxt, 4)
                if last.exists:
                    need(dve, ot_high_done, last.times(1, 1))
                    dve.tensor_tensor(ot_low[:], ps_w[:, 0:2 * NQ].rearrange("p (a t) -> p a t", a=2), ot_high[:],
                                      ALU.subtract).then_inc(ot_low_done, 1)
                if last.exists:
                    need(dve, out_mm, last.times(1, 1))
                    need(dve, xb_done, last.times(1, 1))
                    need(dve, xmid_stored[last.slot], last.uses(16) + -16)
                    dve.tensor_tensor(x_mid[:, last.slot, :], ps_w[0:NQ, 0:C], x_bias[:], ALU.add).then_inc(xmid_done, 1)
                if last.exists:
                    need(dve, xmid_done, last.times(1, 1))
                    need(dve, xn_done, last.times(1))
                    dve.bn_stats(stats[:, 0, :], x_mid[:, last.slot, :]).then_inc(stat_done, 1)
                    need(dve, stat_done, last.times(1, 1))
                reduce_max(nxt, 5)
                if last.exists:
                    dve.bn_aggr(mean_var[:, 0, :], stats[:, 0, :]).then_inc(aggr_done, 1)
                    halve_bits(1, (last.times(1, 1), aggr_done), last.times(1, 1) + NG)
                reduce_max(nxt, 6)
                reduce_max(nxt, 7)

            dve.wait_ge(ones_set, 1)
            steps(dve, step, query_group)

            for g in range(NG):
                for m in range(2):
                    dve.wait_ge(g_relu_done, 2 * g + m + 1)
                    dve.tensor_reduce(h_sums[:, m, g, :], g_relu[:, m, :].rearrange("p (b t) -> p t b", b=GB),
                                      AX_X, ALU.add).then_inc(g_part, 1)
            dve.wait_ge(g_part, 2 * NG)
            dve.tensor_reduce(h_sum[:], h_sums[:].rearrange("p m g t -> p m t g"), AX_X, ALU.add).then_inc(g_sum, 1)

            dve.wait_ge(gates_loaded, 16 * PAT)

            def add_first(e, s, t):
                dve.wait_ge(z1_mm, e * (2 * TT) + (s * TT + t + 1))
                gate_col = gates[:, t % PAT, C + e:C + e + 1] if isinstance(e, int) else \
                    gates[:, t % PAT, bass.ds(e + C, 1)]
                dve.scalar_tensor_tensor(out=acc[:, t, 512 * s:512 * s + 512], in0=banks[:, t % NB1, :],
                                         scalar=gate_col, in1=acc[:, t, 512 * s:512 * s + 512],
                                         op0=ALU.mult, op1=ALU.add).then_inc(acc_done, 1)

            for s in range(2):
                for t in range(TT):
                    if s == 0:
                        dve.wait_ge(acc_loaded[t], 16)
                    add_first(0, s, t)
            with dve.Fori(1, E) as e:
                for s in range(2):
                    for t in range(TT):
                        add_first(e, s, t)

            def add_second(ep, t):
                dve.wait_ge(z2_mm, ep * TT + (t + 1))
                for k in range(2):
                    gate_col = gates[:, t % PAT, C + 2 * ep + k:C + 2 * ep + k + 1] if isinstance(ep, int) else \
                        gates[:, t % PAT, bass.ds(ep * 2 + (C + k), 1)]
                    if k == 1:
                        dve.wait_ge(y_done, ep * (2 * TT) + (2 * t + 1))
                    dve.scalar_tensor_tensor(out=y[:, t, :], in0=banks[:, t % 2, C * k:C * k + C], scalar=gate_col,
                                             in1=y[:, t, :], op0=ALU.mult, op1=ALU.add).then_inc(y_done, 1)

            def hidden_low(t):
                dve.wait_ge(h_high_done, t + 1)
                ps = banks[:, 4 + 2 * (t % 2):6 + 2 * (t % 2), :].rearrange("p k n -> p (k n)")
                dve.scalar_tensor_tensor(out=h_low[:, t].rearrange("p k n -> p (k n)"), in0=ps, scalar=0.0,
                                         in1=h_high[:, t].rearrange("p k n -> p (k n)"),
                                         op0=ALU.max, op1=ALU.subtract).then_inc(h_low_done, 1)

            dve.wait_ge(y_ready, TT // PAT)
            hidden_low(0)
            for t in range(TT):
                if t + 1 < TT:
                    hidden_low(t + 1)
                add_second(0, t)
            with dve.Fori(1, L2P) as ep:
                for t in range(TT):
                    add_second(ep, t)

        @block.tensor
        def _(pe):
            pe.wait_ge(ident_set, 3)
            xqt, w_part = (xqt_high, xqt_low), (w_high, w_low)

            def query_transpose(g):
                pe.wait_ge(q_norm, GB * (g + 1))
                need(pe, q_xlow, g - 1)
                for j in range(GB):
                    for k in range(IT):
                        last = pe.transpose(ps_qt[g % 2][:, k, j * NQ:(j + 1) * NQ], xq[:, g % 2, j, P * k:P * k + P],
                                            ident[0:NQ, 0:NQ])
                last.then_inc(q_tr, 1)

            def query_group(g):
                if g == 0:
                    query_transpose(0)
                    pe.wait_ge(w_low_done[WQ], 1)
                pe.wait_ge(q_xlow, g + 1)
                for m in range(2):
                    need(pe, q_evac, 2 * g + m - 1)
                    three(pe, ps_q[:, m, 0:GW], lambda a, k: w_part[a][:, WQ, k, P * m:P * m + P],
                          lambda a, k: xqt[a][:, g % 2, k, :], IT).then_inc(q_mm, 1)
                if g + 1 < NG:
                    query_transpose(g + 1)
                if g == 0:
                    pe.wait_ge(w_low_done[WK], 1)
                if g == NG - 1:
                    pe.wait_ge(w_low_done[WV], 1)
                    pe.wait_ge(bv_wide_done, 1)
                    for k in range(IT):
                        last = pe.matmul(ps_o[0:NQ, 0:C], bv_wide[:, k, :], w_f32[:, WO, k, :],
                                         start=(k == 0), stop=(k == 1))
                    last.then_inc(bias_mm, 1)
                    pe.wait_ge(ones_set, 2)
                    pe.wait_ge(stack_set, 16)
                    pe.wait_ge(q_evac, 2 * NG)
                    pe.wait_ge(bias_done, 1)
                    for n in (WO, GW1):
                        pe.wait_ge(w_low_done[n], 1)

            c_part = (c_high, c_low)

            def key_project(b, m):
                if not b.exists:
                    return
                if m == 0:
                    need(pe, c_low_done, b.times(1, 1))
                    need(pe, xmid_done, b.times(1, -3))
                    if b.i is None and b.c < 4:
                        need(pe, v_evac, b.times(3, -3))
                else:
                    need(pe, k_evac, b.times(2, 1))
                three(pe, ps_w[:, 0:KVE], lambda a, k: w_part[a][:, WK, k, P * m:P * m + P],
                      lambda a, k: c_part[a][:, b.slot, k, :], IT).then_inc(k_mm, 1)

            def value_project(b, c):
                if not b.exists:
                    return
                n = CHROWS[c]
                if c == 0:
                    need(pe, k_evac, b.times(2, 4))
                    if b.i is None:
                        need(pe, xmid_done, b.times(1, -2))
                elif c == 1:
                    need(pe, v_evac, b.times(3, c))
                    need(pe, xt_low_done, b.times(1, -2))
                else:
                    need(pe, v_evac, b.times(3, c))
                three(pe, ps_w[0:n, 0:C], lambda a, k: c_part[a][:, b.slot, k, P * c:P * c + n],
                      lambda a, k: w_part[a][:, WV, k, :], IT).then_inc(v_mm, 1)

            def max_scores(b, k):
                if not b.exists:
                    return
                if k % 4 == 0:
                    need(pe, stack_loaded[b.slot][k // 4], b.uses(96))
                need(pe, max_red, b.times(8, k - 1))
                if k == 1:
                    need(pe, max_copied, b.times(2))
                if k == 5:
                    need(pe, max_copied, b.times(2, 1))
                for n in range(2):
                    h = 2 * k + n
                    last = pe.matmul(ps_max[k % 2][0:NQ, n, 0:NKV], q_stack[0:QROWS, b.slot, h * NQ:(h + 1) * NQ],
                                     k_stack[0:QROWS, b.slot, h, 0:NKV], start=True, stop=True)
                last.then_inc(max_mm, 1)

            def max_transpose(b, h):
                if not b.exists:
                    return
                need(pe, m2_done, b.times(2, h + 1))
                need(pe, max_red, b.times(8, 8 if h else 4))
                pe.transpose(ps_max_t, max_parts[:, h].rearrange("p a h -> p (a h)"), ident_b[0:NQ, 0:NQ])\
                    .then_inc(max_tr, 1)

            def scores(b, u):
                if not b.exists:
                    return
                quarter, c = u // CH, u % CH
                if u % (2 * CH) == 0:
                    need(pe, max_loaded[u // (2 * CH)], b.times(16, 16))
                need(pe, exp_done, b.times(12, u - 1))
                for n in range(HQ):
                    head = HQ * quarter + n
                    last = pe.matmul(ps_sc[:, u % 2, n * NQ:(n + 1) * NQ],
                                     k_stack[0:SROWS, b.slot, head, P * c:P * c + P],
                                     q_stack[0:SROWS, b.slot, head * NQ:(head + 1) * NQ], start=True, stop=True)
                last.then_inc(sc_mm, 1)

            def weigh_values(b, quarter):
                if not b.exists:
                    return
                need(pe, exp_done, b.times(12, CH * (quarter + 1)))
                if quarter == 0:
                    need(pe, v_evac, b.times(3, 3))
                    need(pe, o_normed, b.times(1))
                for c in range(CH):
                    n = CHROWS[c]
                    for g in range(HQ):
                        last = pe.matmul(ps_o[VW * g:VW * g + VW, quarter * NQ:(quarter + 1) * NQ],
                                         v_ones[0:n, b.slot, c, HQ * quarter + g, :],
                                         probs[0:n, quarter, c, g * NQ:(g + 1) * NQ],
                                         start=(c == 0), stop=(c == CH - 1))
                last.then_inc(pv_mm, 1)

            def output_transpose(b):
                if not b.exists:
                    return
                need(pe, o_copied, b.times(1, 1))
                for hb in range(4):
                    last = pe.transpose(ps_o[0:NQ, P * hb:P * hb + P], o_full[:, hb * NQ:(hb + 1) * NQ], ident[:])
                last.then_inc(o_tr, 1)

            def output_back(b):
                if not b.exists:
                    return
                need(pe, o_normed, b.times(1, 1))
                need(pe, v_evac, b.times(3, 9))
                if b.i is None:
                    need(pe, xt_low_done, b.times(1))
                for k in range(IT):
                    last = pe.transpose(ps_w[:, k * NQ:(k + 1) * NQ],
                                        o_norm[:, HH * k:HH * k + HH, :].rearrange("p h d -> p (h d)"),
                                        ident[0:NQ, 0:NQ])
                last.then_inc(ot_mm, 1)

            def output_project(b):
                if not b.exists:
                    return
                need(pe, ot_low_done, b.times(1, 1))
                ot = (ot_high, ot_low)
                three(pe, ps_w[0:NQ, 0:C], lambda a, k: ot[a][:, k, :], lambda a, k: w_part[a][:, WO, k, :], IT)\
                    .then_inc(out_mm, 1)

            def token_transpose(b):
                if not b.exists:
                    return
                need(pe, xn_done, b.times(1, 1))
                need(pe, v_evac, b.times(3, 10))
                for k in range(IT):
                    last = pe.transpose(ps_w[:, k * NQ:(k + 1) * NQ], x_norm[:, P * k:P * k + P], ident[0:NQ, 0:NQ])
                last.then_inc(xt_mm, 1)

            def step(s):
                old, last, nxt, new = s + -2, s + -1, s + 1, s + 3
                scores(s, 0)
                max_transpose(s, 1)
                weigh_values(last, 3)
                max_scores(nxt, 0)
                value_project(nxt, 0)
                scores(s, 1)
                max_scores(nxt, 1)
                token_transpose(old)
                scores(s, 2)
                output_transpose(last)
                scores(s, 3)
                max_scores(nxt, 2)
                value_project(nxt, 1)
                scores(s, 4)
                max_scores(nxt, 3)
                value_project(nxt, 2)
                scores(s, 5)
                weigh_values(s, 0)
                max_scores(nxt, 4)
                output_back(last)
                scores(s, 6)
                max_transpose(nxt, 0)
                weigh_values(s, 1)
                scores(s, 7)
                output_project(last)
                max_scores(nxt, 5)
                scores(s, 8)
                max_scores(nxt, 6)
                key_project(new, 0)
                scores(s, 9)
                weigh_values(s, 2)
                scores(s, 10)
                max_scores(nxt, 7)
                scores(s, 11)
                key_project(new, 1)

            steps(pe, step, query_group)

            for g in range(NG):
                for m in range(2):
                    n = 2 * g + m
                    need(pe, g_relu_done, n - 1)
                    if n == 0:
                        pe.wait_ge(xt_low_done, B)
                    three(pe, banks[:, m, 0:GW], lambda a, k: w_part[a][:, GW1, k, P * m:P * m + P],
                          lambda a, k: xt_parts[:, a, k, GW * g:GW * g + GW], IT).then_inc(g_mm, 1)
            pe.wait_ge(g_sum, 1)
            for k in range(2):
                last = pe.matmul(banks[0:E, 2, 0:NQ], gw2_sb[:, k, :], h_sum[:, k, :], start=(k == 0), stop=(k == 1))
            last.then_inc(g_gate_mm, 1)
            pe.wait_ge(g_t_done, 1)
            pe.wait_ge(eb_loaded, 32)
            for n in range(3):
                cols = slice(512 * n, min(512 * (n + 1), GCOLS))
                pe.matmul(banks[0:NQ, 3 + n, 0:cols.stop - cols.start], gate_t[:], eb_sb[:, cols],
                          start=True, stop=True).then_inc(g_exp_mm, 1)
            pe.wait_ge(g_row_done, 3)

            def first_layer(e, s, t, first):
                if t == 0:
                    pe.wait_ge(wl_done, e * 2 + (s + 1))
                if not (first and s * TT + t < NB1):
                    pe.wait_ge(acc_done, e * (2 * TT) + (s * TT + t - NB1 + 1))
                three(pe, banks[:, t % NB1, :], lambda a, k: xt_parts[:, a, k, P * t:P * t + P],
                      lambda a, k: w1_parts[:, s, a, k, :], IT).then_inc(z1_mm, 1)

            for s in range(2):
                for t in range(TT):
                    first_layer(0, s, t, True)
            with pe.Fori(1, E) as e:
                for s in range(2):
                    for t in range(TT):
                        first_layer(e, s, t, False)

            def hidden_transpose(t):
                pe.wait_ge(acc_done, 2 * TT * (E - 1) + TT + t + 1)
                if t < 2:
                    pe.wait_ge(acc_done, 2 * TT * E)
                else:
                    pe.wait_ge(h_low_done, t - 1)
                for k in range(OT):
                    last = pe.transpose(banks[:, 4 + 2 * (t % 2) + k // 4, P * (k % 4):P * (k % 4) + P],
                                        acc[:, t, P * k:P * k + P], ident[:])
                last.then_inc(h_tr, 1)

            h_part = (h_high, h_low)

            def second_layer(ep, slot, t, first):
                if first:
                    pe.wait_ge(h_low_done, t + 1)
                if not (first and t < 2):
                    pe.wait_ge(y_done, ep * (2 * TT) + 2 * (t - 1))
                n = 0
                for c in range(L2C):
                    if t == 0:
                        pe.wait_ge(wl_done, ep * L2C + (L1N + c + 1))
                    for a, b in ((0, 0), (0, 1), (1, 0)):
                        for k in range(2):
                            w = w2_parts[:, slot, c, b, k, :]
                            last = pe.matmul(banks[:, t % 2, :], h_part[a][:, t, 2 * c + k, :], w,
                                             start=(n == 0), stop=(n == 3 * OT - 1))
                            n += 1
                last.then_inc(z2_mm, 1)

            hidden_transpose(0)
            for t in range(TT):
                if t + 1 < TT:
                    hidden_transpose(t + 1)
                second_layer(0, 0, t, True)
            with pe.Fori(1, L2P) as ep:
                for t in range(TT):
                    second_layer(ep, bass.ds(ep % 2, 1), t, False)


def kernel(x, ctx_1024, L0_xattn_w_q, L0_xattn_b_q, L0_xattn_w_kv, L0_xattn_b_kv, L0_xattn_w_out, L0_xattn_b_out,
           L0_ffn_gW1, L0_ffn_gb1, L0_ffn_gW2, L0_ffn_gb2, L0_ffn_eW1, L0_ffn_eb1, L0_ffn_eW2, L0_ffn_eb2):
    import numpy as np
    import concourse.bacc as bacc
    from concourse.bass_utils import run_bass_kernel_spmd

    def a(v):
        return np.asarray(v)

    order = np.array([(2 * (p % HH) + m) * D + p // HH for m in range(2) for p in range(P)])
    w_kv, b_kv = a(L0_xattn_w_kv), a(L0_xattn_b_kv)

    def tiles(w):
        return w.reshape(IT, P, -1).transpose(1, 0, 2)

    def halves(v):
        return v.reshape(2, P).T

    e1, e2 = a(L0_ffn_eW1), a(L0_ffn_eW2)
    arrays = {
        "x": a(x),
        "ctx_t": a(ctx_1024).transpose(2, 0, 1).reshape(IT, P, B, NKV).transpose(1, 2, 0, 3),
        "wq": tiles(a(L0_xattn_w_q)[:, order]), "wk": tiles(w_kv[:, :C][:, order]),
        "wv": tiles(w_kv[:, C:]), "wo": tiles(a(L0_xattn_w_out)), "bo": a(L0_xattn_b_out).reshape(1, C),
        "gw1": tiles(a(L0_ffn_gW1).T), "gb2": a(L0_ffn_gb2).reshape(E, 1),
        "small": np.concatenate([halves(a(L0_xattn_b_q)[order]), halves(b_kv[:C][order]), halves(b_kv[C:]),
                                 halves(a(L0_ffn_gb1)), a(L0_ffn_gW2).reshape(E, 2, P).transpose(2, 1, 0)
                                 .reshape(P, 2 * E)], axis=1),
        "w1": e1.reshape(E, 2, 512, IT, P).transpose(0, 1, 4, 3, 2).reshape(2 * E, P, IT, 512),
        "eb": np.concatenate([a(L0_ffn_eb1), a(L0_ffn_eb2)], axis=1),
        "w2": e2.reshape(E // 2, 2, C, OT // 2, 2, P).transpose(0, 3, 5, 4, 1, 2).reshape(2 * E, P, 2, 512),
    }
    arrays = {k: np.ascontiguousarray(v) for k, v in arrays.items()}
    nc = bacc.Bacc("TRN2", target_bir_lowering=False, num_devices=1)
    args = {k: nc.dram_tensor(f"in_{k}", v.shape, mybir.dt.from_np(v.dtype), kind="ExternalInput").ap()
            for k, v in arrays.items()}
    out = nc.dram_tensor("out", (T, C), F32, kind="ExternalOutput").ap()
    build(nc, out=out, **args)
    r = run_bass_kernel_spmd(nc, [{f"in_{k}": v for k, v in arrays.items()}], core_ids=[0])
    return r.results[0]["out"].reshape(B, NQ, C)
```

```python
from contextlib import ExitStack

import concourse.bass as bass
from concourse import mybir

F32 = mybir.dt.float32
F32R = mybir.dt.float32r
BF16 = mybir.dt.bfloat16
I32 = mybir.dt.int32
ALU = mybir.AluOpType
ACT = mybir.ActivationFunctionType
AX_X = mybir.AxisListType.X

P = 128
B, NQ, C = 16, 112, 256
NKV = 375
KVE = NKV + 1
KVP = 384
CH = KVP // P
CHROWS = [P, P, NKV - 2 * P]
H, D = 16, 16
HH = H // 2
HQ = H // 4
SCALE = float(D) ** -0.5
EPS = 1e-5
MAGIC = 0x5EF759DF
ROOT_STEPS = 3
ROOTS = 3
ROOT_OPS = 1 + 4 * ROOT_STEPS
T = B * NQ
TT = T // P
PAT = NQ // 16
DFF, E = 1024, 8
IT = C // P
OT = DFF // P
GB = 4
NG = B // GB
GW = GB * NQ
VW = 2 * D
GCOLS = DFF + C + E
QROWS = 6 * D
SROWS = QROWS + 2


class Batch:

    def __init__(self, c, i=None):
        self.c, self.i = c, i

    def __add__(self, n):
        return Batch(self.c + n, self.i)

    @property
    def exists(self):
        return self.i is not None or 0 <= self.c < B

    def exists_from(self, first):
        return self.exists and (self.i is not None or self.c >= first)

    @property
    def slot(self):
        return self.c % 2

    def times(self, per, more=0, of=B):
        if self.i is None:
            return min(per * self.c + more, per * of)
        return self.i * (2 * per) + (per * self.c + more)

    def uses(self, per):
        if self.i is None:
            return per * (self.c // 2 + 1)
        return self.i * per + per * (self.c // 2 + 1)


FIRST_STEP, LOOP_STEP, LOOPS, LAST_STEP = -1, 2, 5, 17
EARLY = 3


def steps(eng, step):
    for s in range(FIRST_STEP, LOOP_STEP):
        step(Batch(s))
    with eng.Fori(0, LOOPS) as i:
        for s in range(LOOP_STEP, LOOP_STEP + 2):
            step(Batch(s, i))
    for s in range(LOOP_STEP + 2 * LOOPS, LAST_STEP + 1):
        step(Batch(s))


def need(eng, sem, value):
    if isinstance(value, int) and value <= 0:
        return
    eng.wait_ge(sem, value)


def build(nc, x, ctx_t, wq, wk, wv, wo, bo, gw1, small, gb2, w1, eb, w2, out):
    with ExitStack() as stack:
        def psum(name, shape, dt=F32):
            return stack.enter_context(nc.psum_tensor(name, shape, dt))

        def sem(name):
            return stack.enter_context(nc.semaphore(name))

        def size(shape, dt):
            n = 2 if dt == BF16 else 4
            for d in shape[1:]:
                n *= d
            return n

        class Region:

            def __init__(self, start, end):
                self.at, self.end = start, end

            def take(self, name, shape, dt):
                t = nc.alloc_sbuf_tensor_at(name, shape, dt, offset=self.at)
                self.at += (size(shape, dt) + 31) // 32 * 32
                assert self.at <= self.end, (name, self.at, self.end)
                return t

        start = (nc.sbuf_base + 31) // 32 * 32
        RAW = 2 * IT * 512 * 4
        W1B = 2 * 2 * IT * 512 * 4
        XTB = 2 * IT * T * 4
        W2B = 2 * 2 * OT * 512 * 4
        at_w2 = start + RAW
        at_w1 = at_w2 + W2B - XTB - W1B
        at_xt = at_w1 + W1B
        at_main = at_xt + XTB

        w_raw = nc.alloc_sbuf_tensor_at("w_raw", [P, 2, IT, 512], F32, offset=start)
        w1_parts = nc.alloc_sbuf_tensor_at("w1_parts", [P, 2, 2, IT, 512], F32R, offset=at_w1)
        xt_parts = nc.alloc_sbuf_tensor_at("xt_parts", [P, 2, IT, T], F32R, offset=at_xt)
        w2_parts = nc.alloc_sbuf_tensor_at("w2_parts", [P, 2, OT // 2, 2, 2, 512], F32R, offset=at_w2)

        ffn = Region(at_main, nc.sbuf_usable_end)
        gates = ffn.take("gates", [P, PAT, C + E], F32)
        y = ffn.take("y", [P, TT, C], F32)
        at_acc = ffn.at
        acc = ffn.take("acc", [P, TT, DFF], F32)
        h_high = nc.alloc_sbuf_tensor_at("h_high", [P, TT, OT, P], F32R, offset=at_acc)
        b1_rows = nc.alloc_sbuf_tensor_at("b1_rows", [P, PAT, DFF], F32, offset=ffn.at)
        h_low = ffn.take("h_low", [P, TT, OT, P], F32R)
        keep = Region(ffn.at, nc.sbuf_usable_end)
        ident = keep.take("ident", [P, P], F32)
        ident_b = keep.take("ident_b", [P, P], BF16)
        ident_e = keep.take("ident_e", [E, E], F32)
        small_sb = keep.take("small_sb", [P, 8 + 2 * E], F32)
        bq_sb, bk_sb, bv_sb, gb1_sb = (small_sb[:, 2 * n:2 * n + 2] for n in range(4))
        gw2_sb = small_sb[:, 8:8 + 2 * E].rearrange("p (k e) -> p k e", k=2)
        gb2_sb = keep.take("gb2_sb", [E, 1], F32)
        gate_t = keep.take("gate_t", [E, P], F32)
        max_rows = keep.take("max_rows", [D, 2, NQ], BF16)
        stats = keep.take("stats", [NQ, 6], F32)
        mean_var = keep.take("mean_var", [NQ, B, 2], F32)
        half_var = keep.take("half_var", [NQ, B], F32)
        magic = keep.take("magic", [NQ, B], I32)
        one_half = keep.take("one_half", [NQ, B], F32)
        half_bits = keep.take("half_bits", [NQ, B], I32)
        root_tmp = keep.take("root_tmp", [NQ, B], F32)
        rstd = keep.take("rstd", [NQ, B], F32)
        maxima = keep.take("maxima", [NQ, 2, H], F32)
        max_parts = keep.take("max_parts", [NQ, 2, 2, HH], BF16)
        recip = keep.take("recip", [NQ, H], F32)

        front = Region(at_w2, at_w1)
        k_f32 = front.take("k_f32", [P, 2, KVE], F32)
        k_rest = front.take("k_rest", [P, 2, KVE], F32)
        k_parts = front.take("k_parts", [P, 3, 2, KVP], BF16)
        o_full = front.take("o_full", [P, 4 * NQ], F32)
        o_norm = front.take("o_norm", [NQ, H, D], F32)
        ot_high = front.take("ot_high", [P, 2, NQ], F32R)
        ot_low = front.take("ot_low", [P, 2, NQ], F32R)
        x_norm = front.take("x_norm", [NQ, C], F32)
        x_bias = front.take("x_bias", [NQ, C], F32)
        x_mid = front.take("x_mid", [NQ, 2, C], F32)

        main = Region(at_main, ffn.at)
        w_f32 = main.take("w_f32", [P, 5, IT, C], F32)
        w_high = main.take("w_high", [P, 5, IT, C], F32R)
        w_low = main.take("w_low", [P, 5, IT, C], F32R)
        x_all = main.take("x_all", [NQ, B, C], F32)
        at_probs = main.at
        probs = main.take("probs", [P, 4, CH, HQ * NQ], F32)
        v_ones = main.take("v_ones", [P, 2, CH, H, VW], F32)
        q_stack = main.take("q_stack", [P, 2, H * NQ], BF16)
        k_stack = main.take("k_stack", [P, 2, H, KVP], BF16)
        at_ctx = main.at
        c_raw = main.take("c_raw", [P, 2, IT, KVE], F32)
        c_high = main.take("c_high", [P, 2, IT, KVE], F32R)
        c_low = main.take("c_low", [P, 2, IT, KVE], F32R)
        bias_row = main.take("bias_row", [NQ, C], F32)
        bo_row = main.take("bo_row", [NQ, C], F32)
        bv_wide = main.take("bv_wide", [P, 2, NQ], F32)
        gate = Region(at_ctx, main.at)
        g_relu = gate.take("g_relu", [P, 2, GW], F32)
        h_sums = gate.take("h_sums", [P, 2, NG, NQ], F32)
        eb_sb = gate.take("eb_sb", [E, GCOLS], F32)
        pre = Region(at_w1, at_main)
        xq = pre.take("xq", [NQ, 2, GB, C], F32)
        xqt_high = pre.take("xqt_high", [P, 2, IT, GW], F32R)
        xqt_low = pre.take("xqt_low", [P, 2, IT, GW], F32R)
        q_f32 = pre.take("q_f32", [P, 2, GB, 2, NQ], F32)
        q_rest = pre.take("q_rest", [P, GB, 2, NQ], F32)
        q_stats = pre.take("q_stats", [NQ, B, 6], F32)
        minus_ones = pre.take("minus_ones", [P, 2 * 2 * H * KVP // P], BF16)

        q_parts = [nc.alloc_sbuf_tensor_at(f"q_parts{g}", [P, 3, GB, 2, NQ], BF16, offset=at)
                   for g, at in enumerate((at_probs, pre.at, start, at_w1))]
        assert size([P, 3, GB, 2, NQ], BF16) <= min(RAW, at_main - pre.at, size([NQ, 2, GB, C], F32))

        WQ, WK, WV, WO, GW1 = range(5)

        k_dram = nc.dram_tensor("k_dram", [2, 3, D, H * KVP], BF16, kind="Internal").ap()
        q_dram = nc.dram_tensor("q_dram", [B, 3, D, H * NQ], BF16, kind="Internal").ap()
        xmid_dram = nc.dram_tensor("xmid_dram", [T, C], F32, kind="Internal").ap()
        gate_dram = nc.dram_tensor("gate_dram", [2 * NQ, GCOLS], F32, kind="Internal").ap()

        banks = psum("banks", [P, 8, 512])
        ps_max = [banks[:, 0:2, :], banks[:, 2:4, :]]
        ps_max_t = banks[0:D, 2, 384:448].bitcast(BF16)[:, 0:NQ]
        ps_sc = banks[:, 4:6, :]
        ps_qt = [banks[:, 0:2, :], banks[:, 2:4, :]]
        ps_q = banks[:, 4:6, :]
        ps_o = banks[:, 6, :]
        ps_w = banks[:, 7, :]
        ps_xt = banks[:, 7, C:C + 2 * NQ]

        x_loaded = [sem(f"x_loaded{g}") for g in range(NG)]
        w_loaded = [sem(f"w_loaded{n}") for n in range(5)]
        small_loaded, late_loaded = sem("small_loaded"), sem("late_loaded")
        ones_set, zero_set, ident_set = sem("ones_set"), sem("zero_set"), sem("ident_set")
        minus_set = sem("minus_set")
        stack_set, pad_set = sem("stack_set"), sem("pad_set")
        w_high_done = sem("w_high_done")
        w_low_done = [sem(f"w_low_done{n}") for n in range(5)]
        bv_wide_done, bias_mm, bias_done = sem("bv_wide_done"), sem("bias_mm"), sem("bias_done")
        q_stat, q_aggr, q_norm = sem("q_stat"), sem("q_aggr"), sem("q_norm")
        root_set, eps_added, bits_halved, root_done = sem("root_set"), sem("eps_added"), sem("bits_halved"), sem("root_done")
        q_tr, q_xhigh, q_xlow, q_mm = sem("q_tr"), sem("q_xhigh"), sem("q_xlow"), sem("q_mm")
        q_evac, qr_done, q2_done, q3_done = sem("q_evac"), sem("qr_done"), sem("q2_done"), sem("q3_done")
        q_first_stored = sem("q_first_stored")
        q_stored = [sem(f"q_stored{g}") for g in range(NG)]
        c_loaded = [sem("c_loaded0"), sem("c_loaded1")]
        c_high_done, c_low_done = sem("c_high_done"), sem("c_low_done")
        k_mm, v_mm, k_evac, v_evac = sem("k_mm"), sem("v_mm"), sem("k_evac"), sem("v_evac")
        k1_done, kr_done, k2_done, k3_done = sem("k1_done"), sem("kr_done"), sem("k2_done"), sem("k3_done")
        k_stored = sem("k_stored")
        stack_loaded = [[sem(f"stack_loaded{s}{h}") for h in range(2)] for s in range(2)]
        max_mm, max_red, m1_done, m2_done = sem("max_mm"), sem("max_red"), sem("m1_done"), sem("m2_done")
        max_tr, max_copied = sem("max_tr"), sem("max_copied")
        max_loaded = [sem("max_loaded0"), sem("max_loaded1")]
        sc_mm, exp_done, pv_mm = sem("sc_mm"), sem("exp_done"), sem("pv_mm")
        o_copied, o_tr, recip_done, o_normed = sem("o_copied"), sem("o_tr"), sem("recip_done"), sem("o_normed")
        ot_mm, ot_high_done, ot_low_done, out_mm = (
            sem("ot_mm"), sem("ot_high_done"), sem("ot_low_done"), sem("out_mm"))
        xb_done, xmid_done, stat_done, aggr_done = (
            sem("xb_done"), sem("xmid_done"), sem("stat_done"), sem("aggr_done"))
        xn_done, xt_mm, xt_high_done, xt_low_done = (
            sem("xn_done"), sem("xt_mm"), sem("xt_high_done"), sem("xt_low_done"))
        xmid_stored = [sem("xmid_stored0"), sem("xmid_stored1")]
        eb_loaded, g_mm, g_relu_done, g_part = sem("eb_loaded"), sem("g_mm"), sem("g_relu_done"), sem("g_part")
        g_gate_mm, g_t_done, g_exp_mm = sem("g_gate_mm"), sem("g_t_done"), sem("g_exp_mm")
        g_row_done = sem("g_row_done")
        g_stored = [sem(f"g_stored{n}") for n in range(3)]
        rows_loaded = [[sem(f"rows_loaded{h}_{p}") for p in range(PAT)] for h in range(2)]
        y_loaded, y_ready = sem("y_loaded"), sem("y_ready")
        raw_loaded = [sem("raw_loaded0"), sem("raw_loaded1")]
        wh_done, wl_done = sem("wh_done"), sem("wl_done")
        z1_mm, acc_done = sem("z1_mm"), sem("acc_done")
        h_tr, h_high_done, h_low_done = sem("h_tr"), sem("h_high_done"), sem("h_low_done")
        z2_mm, y_done, out_stored = sem("z2_mm"), sem("y_done"), sem("out_stored")

        def three(pe, out_ap, left, right, tiles, stop_last=True):
            n = 0
            for a, b in ((0, 0), (0, 1), (1, 0)):
                for k in range(tiles):
                    last = pe.matmul(out_ap, left(a, k), right(b, k), start=(n == 0), stop=(n == 3 * tiles - 1))
                    n += 1
            return last

        def queries_stored(eng, g):
            if g == 0:
                eng.wait_ge(q_first_stored, 16)
            eng.wait_ge(q_stored[g], 16 * (GB - 1 if g == 0 else GB))

        L1N = 2 * E
        L2P = E // 2
        L2C = OT // 2
        NB1 = 7
        GATE_STEP = B - 1
        GATE_BANKS = [0, 1, 2, 3, 0, 1, 4, 5]

        ROW_PARTS = [(DFF, GCOLS), (0, 512), (512, DFF)]
        ROW_BANKS = [7, 6, 7]

        def row_part(p, n):
            start, end = ROW_PARTS[n]
            return b1_rows[:, p, start:end] if end <= DFF else gates[:, p, :]

        block = stack.enter_context(nc.Block())

        @block.sync
        def _(sp):
            def load_x(g):
                sp.dma_start(x_all[:, GB * g:GB * g + GB, :],
                             x[GB * g:GB * g + GB].rearrange("b q c -> q b c")).then_inc(x_loaded[g], 16)

            def load_w(n, w):
                sp.dma_start(w_f32[:, n], w).then_inc(w_loaded[n], 16)

            def load_context(b):
                if not b.exists:
                    return
                need(sp, c_high_done, b.times(1, -1))
                need(sp, c_low_done, b.times(1, -1))
                dram = ctx_t[:, b.times(1), :, :] if b.i is None else ctx_t[:, bass.ds(b.times(1), 1), :, :]
                sp.dma_start(c_raw[:, b.slot, :, 0:NKV], dram).then_inc(c_loaded[b.slot], 16)

            def load_queries(b, h):
                if b.i is None and b.c < NG:
                    sp.wait_ge(q_first_stored, 16)
                    if b.c > 0:
                        queries_stored(sp, 0)
                elif b.i is not None and h == 0:
                    queries_stored(sp, 2)
                    queries_stored(sp, 3)
                need(sp, sc_mm, b.times(12, -24 + 6 * (h + 1)))
                cols = slice(h * HH * NQ, (h + 1) * HH * NQ)
                q = q_dram[b.times(1)] if b.i is None else q_dram[bass.ds(b.times(1), 1)].rearrange("a p d t -> (a p) d t")
                for row, part, reps in ((0, 0, 3), (3 * D, 1, 2), (5 * D, 2, 1)):
                    src = q[part:part + 1, :, cols].to_broadcast([reps, D, HH * NQ])
                    sp.dma_start(q_stack[row:row + reps * D, b.slot, cols], src).then_inc(stack_loaded[b.slot][h], 16)

            def load_keys(b, h):
                need(sp, k_stored, b.times(16, 16))
                need(sp, sc_mm, b.times(12, -24 + 6 * (h + 1)))
                k = k_dram[b.slot]
                for row, parts in ((0, 3), (3 * D, 2), (5 * D, 1)):
                    sp.dma_start(
                        k_stack[row:row + parts * D, b.slot, h * HH:(h + 1) * HH, :].rearrange("p h t -> p (h t)"),
                        k[0:parts, :, h * HH * KVP:(h + 1) * HH * KVP].rearrange("p d t -> (p d) t"),
                    ).then_inc(stack_loaded[b.slot][h], 16)

            def load_maxima(b, h):
                need(sp, max_copied, b.times(2, h + 1))
                sp.dma_start(q_stack[QROWS:SROWS, b.slot, h * HH * NQ:(h + 1) * HH * NQ],
                             max_rows[:, h, :]).then_inc(max_loaded[h], 16)

            def store_keys(b):
                for h in range(2):
                    need(sp, stack_loaded[b.slot][h], b.uses(96) + -96)
                need(sp, k3_done, b.times(1, 1))
                sp.dma_start(k_dram[b.slot].rearrange("p d (h t) -> (d h) p t", h=HH),
                             k_parts[:].rearrange("p k m t -> p k (m t)")).then_inc(k_stored, 16)

            def store_queries(g, batches, stored):
                sp.wait_ge(q3_done, g + 1)
                for j in batches:
                    sp.dma_start(q_dram[GB * g + j].rearrange("p d (h t) -> (d h) p t", h=HH),
                                 q_parts[g][:, :, j].rearrange("p k m t -> p k (m t)")).then_inc(stored, 16)

            load_x(0)
            load_w(WQ, wq)
            load_x(1)
            sp.wait_ge(pad_set, 1)
            load_context(Batch(0))
            load_w(WK, wk)
            load_x(2)
            load_x(3)
            sp.dma_start(small_sb[:], small).then_inc(small_loaded, 16)
            load_context(Batch(1))
            load_w(WV, wv)
            sp.wait_ge(minus_set, 1)
            sp.dma_start(k_stack[QROWS:SROWS].rearrange("p s h t -> p (s h t)"), minus_ones[:]).then_inc(stack_set, 16)
            load_w(WO, wo)
            sp.dma_start(bo_row[:], bo.to_broadcast([NQ, C])).then_inc(late_loaded, 16)
            sp.dma_start(gb2_sb[:], gb2).then_inc(late_loaded, 16)
            load_w(GW1, gw1)
            load_context(Batch(2))
            store_queries(0, range(1), q_first_stored)
            store_keys(Batch(0))
            for h in range(2):
                load_queries(Batch(0), h)
                load_keys(Batch(0), h)
            store_queries(0, range(1, GB), q_stored[0])
            load_context(Batch(3))
            store_queries(1, (0, 1), q_stored[1])
            load_maxima(Batch(0), 0)
            store_keys(Batch(1))
            load_queries(Batch(1), 0)
            store_queries(1, (2,), q_stored[1])
            load_keys(Batch(1), 0)
            load_maxima(Batch(0), 1)
            for load in (load_queries, load_keys):
                load(Batch(1), 1)

            def step(s):
                if s.i is None and s.c == FIRST_STEP:
                    return
                if (s + -2).exists:
                    b = s + -2
                    need(sp, xmid_done, b.times(1, 1))
                    dst = xmid_dram.rearrange("(b q) c -> b q c", q=NQ)
                    dst = dst[b.times(1)] if b.i is None else dst[bass.ds(b.times(1), 1)].rearrange("a q c -> (a q) c")
                    sp.dma_start(dst, x_mid[:, b.slot, :]).then_inc(xmid_stored[b.slot], 16)
                b = s + 1
                if b.exists_from(2):
                    load_queries(b, 1)
                    load_keys(b, 1)
                if s.exists_from(1):
                    load_maxima(s, 1)
                load_context(s + 4)
                if s.i is None and s.c == 1:
                    store_queries(2, (2, 3), q_stored[2])
                b = s + 2
                if b.exists:
                    store_keys(b)
                    load_queries(b, 0)
                if (s + 1).exists:
                    load_maxima(s + 1, 0)
                if s.i is None and s.c == 0:
                    store_queries(1, (3,), q_stored[1])
                if s.i is None and s.c == 1:
                    store_queries(3, (0,), q_stored[3])
                if b.exists:
                    load_keys(b, 0)
                if s.i is None and s.c == GATE_STEP:
                    sp.wait_ge(c_low_done, B)
                    sp.wait_ge(v_mm, CH * B)
                    sp.wait_ge(ident_set, 3)
                    sp.dma_start(eb_sb[:, 0:DFF + C], eb).then_inc(eb_loaded, 16)
                    sp.dma_start(eb_sb[:, DFF + C:GCOLS], ident_e[:]).then_inc(eb_loaded, 16)
                if s.i is None and s.c == 0:
                    store_queries(2, (0, 1), q_stored[2])
                if s.i is None and s.c == 1:
                    store_queries(3, range(1, GB), q_stored[3])
                    queries_stored(sp, 1)
                if s.i is None and s.c == LOOP_STEP + 2 * LOOPS:
                    for n in range(2):
                        sp.dma_start(w_raw[:, n], w1[n]).then_inc(raw_loaded[n], 16)

            steps(sp, step)

            def load_raw(freed, slot, src):
                sp.wait_ge(wl_done, freed)
                sp.dma_start(w_raw[:, slot], src).then_inc(raw_loaded[slot], 16)

            for n in range(2):
                load_raw(n + 1, n, w1[2 + n])

            for n, (start, end) in enumerate(ROW_PARTS):
                sp.wait_ge(g_row_done, n + 1)
                sp.dma_start(gate_dram.rearrange("(k q) c -> q k c", k=2)[:, :, start:end],
                             row_part(0, n)[0:NQ].unsqueeze(1).to_broadcast([NQ, 2, end - start])).then_inc(g_stored[n], 16)
            for n, (start, end) in enumerate(ROW_PARTS):
                if n == 1:
                    continue
                sp.wait_ge(g_stored[n], 16)
                if n == 0:
                    sp.wait_ge(g_stored[1], 16)
                for p in range(1, PAT):
                    for k in range(n, 2) if n == 0 else (2,):
                        start, end = ROW_PARTS[k]
                        sp.dma_start(row_part(p, k), gate_dram[16 * p:16 * p + P, start:end])\
                            .then_inc(rows_loaded[k // 2][p], 16)
            for s in range(2):
                sp.wait_ge(xmid_stored[s], 16 * B // 2)
            sp.dma_start(y[:], xmid_dram.rearrange("(t p) c -> p t c", p=P)).then_inc(y_loaded, 16)

            with sp.Fori(2, E) as e:
                for n in range(2):
                    load_raw(e * 2 + (n - 1), n, w1[bass.ds(e * 2 + n, 1)].rearrange("a p k n -> (a p) k n"))
            with sp.Fori(0, L2P) as ep:
                for c in range(L2C):
                    load_raw(ep * L2C + (L1N + c - 1), c % 2,
                             w2[bass.ds(ep * L2C + c, 1)].rearrange("a p k n -> (a p) k n"))

            outs = out.rearrange("(t p) c -> t p c", p=P)
            for t in range(TT):
                sp.wait_ge(y_done, 2 * (TT * (L2P - 1) + t + 1))
                sp.dma_start(outs[t], y[:, t, :]).then_inc(out_stored, 16)
            sp.wait_ge(out_stored, 16 * TT)

        @block.gpsimd
        def _(pool):
            pool.memset(c_raw[:, :, :, NKV:KVE], 0.0).then_inc(pad_set, 1)
            pool.memset(ident[:], 0.0).then_inc(zero_set, 1)
            pool.memset(ident_b[:], 0.0).then_inc(zero_set, 1)
            pool.memset(ident_e[:], 0.0).then_inc(zero_set, 1)
            pool.wait_ge(zero_set, 3)
            for m, n in ((ident, P), (ident_b, P), (ident_e, E)):
                pool.affine_select(out=m[:], in_=m[:], compare_op=ALU.not_equal, fill=1.0, base=0,
                                   pattern=[[-1, n]], channel_multiplier=1).then_inc(ident_set, 1)
            pool.memset(magic[:], MAGIC)
            pool.memset(one_half[:], 1.5).then_inc(root_set, 1)
            pool.wait_ge(root_set, 1)
            pool.memset(minus_ones[:], -1.0).then_inc(minus_set, 1)
            pool.memset(k_parts[:, :, :, KVE:KVP], 0.0).then_inc(ones_set, 1)
            pool.memset(v_ones[:, :, :, :, D:VW], 1.0).then_inc(ones_set, 1)

            def inverse_root(start, end, before):
                n = slice(start, end)
                y, t = rstd[:, n], root_tmp[:, n]
                pool.tensor_tensor(y.bitcast(I32), magic[:, n], half_bits[:, n], ALU.subtract).then_inc(root_done, 1)
                for k in range(ROOT_STEPS):
                    pool.wait_ge(root_done, before + (4 * k + 1))
                    pool.tensor_tensor(t, y, y, ALU.mult).then_inc(root_done, 1)
                    pool.wait_ge(root_done, before + (4 * k + 2))
                    pool.tensor_tensor(t, t, half_var[:, n], ALU.mult).then_inc(root_done, 1)
                    pool.wait_ge(root_done, before + (4 * k + 3))
                    pool.tensor_tensor(t, one_half[:, n], t, ALU.subtract).then_inc(root_done, 1)
                    pool.wait_ge(root_done, before + (4 * k + 4))
                    pool.tensor_tensor(y, y, t, ALU.mult).then_inc(root_done, 1)

            def key_rest(b):
                need(pool, k1_done, b.times(1, 1))
                pool.tensor_tensor(k_rest[:], k_f32[:], k_parts[:, 0, :, 0:KVE], ALU.subtract).then_inc(kr_done, 1)

            def key_third(b):
                need(pool, k2_done, b.times(1, 1))
                pool.tensor_tensor(k_parts[:, 2, :, 0:KVE], k_rest[:], k_parts[:, 1, :, 0:KVE], ALU.subtract)\
                    .then_inc(k3_done, 1)

            def context_low(b):
                need(pool, c_high_done, b.times(1, 1))
                pool.tensor_tensor(c_low[:, b.slot], c_raw[:, b.slot], c_high[:, b.slot], ALU.subtract)\
                    .then_inc(c_low_done, 1)

            def query_rest(g):
                pool.wait_ge(q_evac, 2 * (g + 1))
                need(pool, q3_done, g)
                pool.tensor_tensor(q_rest[:], q_f32[:, g % 2], q_parts[g][:, 0], ALU.subtract).then_inc(qr_done, 1)

            def low_part(r, slot, dst):
                pool.wait_ge(wh_done, r)
                pool.tensor_tensor(dst(1), w_raw[:, slot], dst(0), ALU.subtract).then_inc(wl_done, 1)

            pool.wait_ge(bits_halved, 1)
            inverse_root(0, GB, 0)
            context_low(Batch(0))
            pool.wait_ge(bits_halved, 2)
            inverse_root(GB, 2 * GB, ROOT_OPS)
            pool.wait_ge(bits_halved, 3)
            inverse_root(2 * GB, B, 2 * ROOT_OPS)
            context_low(Batch(1))
            key_rest(Batch(0))
            query_rest(0)
            key_third(Batch(0))
            for g in range(1, NG):
                if g == NG - 1:
                    context_low(Batch(2))
                query_rest(g)

            def step(s):
                b = s + 2
                if b.exists_from(1):
                    key_rest(b)
                    key_third(b)
                if s.i is None and s.c == FIRST_STEP:
                    context_low(Batch(3))
                b = s + -1
                if b.exists:
                    if b.i is None and b.c == 0:
                        pool.wait_ge(bias_done, 1)
                    need(pool, xmid_done, b.times(1, 0))
                    src = x_all[:, b.times(1), :] if b.i is None else x_all[:, bass.ds(b.times(1), 1), :]
                    pool.tensor_tensor(x_bias[:], src, bias_row[:], ALU.add).then_inc(xb_done, 1)
                b = s + 3
                if b.exists_from(EARLY + 1):
                    context_low(b)
                if s.i is None and s.c == B:
                    low_part(1, 0, lambda part: w1_parts[:, 0, part])
                b = s + -1
                if b.exists:
                    need(pool, bits_halved, b.times(1, 1) + ROOTS)
                    inverse_root(0, 1, b.times(ROOT_OPS) + ROOT_OPS * ROOTS)
                if s.i is None and s.c == B:
                    low_part(2, 1, lambda part: w1_parts[:, 1, part])

            steps(pool, step)

            def first_low(e):
                for s in range(2):
                    low_part(e * 2 + s + 1, s, lambda part: w1_parts[:, s, part])

            first_low(1)
            pool.wait_ge(y_loaded, 16)
            pool.wait_ge(g_row_done, 3)
            for p in range(1, PAT):
                pool.wait_ge(rows_loaded[0][p], 32)
            for n in range(TT // PAT):
                rows = slice(n * PAT, (n + 1) * PAT)
                pool.tensor_tensor(y[:, rows, :], y[:, rows, :], gates[:, :, 0:C], ALU.add).then_inc(y_ready, 1)
            with pool.Fori(2, E) as e:
                first_low(e)
            with pool.Fori(0, L2P) as ep:
                for c in range(L2C):
                    low_part(ep * L2C + (L1N + c + 1), c % 2,
                             lambda part: w2_parts[:, bass.ds(ep % 2, 1), c, part].rearrange("p s a n -> p (s a) n"))

        @block.scalar
        def _(act):
            def weight_high(n):
                act.wait_ge(w_loaded[n], 16)
                act.activation(w_high[:, n], w_f32[:, n], ACT.Copy).then_inc(w_high_done, 1)

            def query_high(g):
                act.wait_ge(q_tr, g + 1)
                need(act, q_mm, 2 * (g - 1))
                act.activation(xqt_high[:, g % 2], ps_qt[g % 2][:, :, 0:GW], ACT.Copy).then_inc(q_xhigh, 1)

            def query_evac(g, m):
                if m == 0:
                    need(act, qr_done, g - 1)
                act.wait_ge(q_mm, 2 * g + m + 1)
                ps = ps_q[:, m, 0:GW].rearrange("p (b t) -> p b t", b=GB)
                act.activation(q_f32[:, g % 2, :, m, :], ps, ACT.Identity, bias=bq_sb[:, m:m + 1])
                act.activation(q_parts[g][:, 0, :, m, :], ps, ACT.Identity, bias=bq_sb[:, m:m + 1])\
                    .then_inc(q_evac, 1)

            def context_high(b):
                need(act, c_loaded[b.slot], b.uses(16))
                need(act, v_mm, b.times(3, -3))
                act.activation(c_high[:, b.slot], c_raw[:, b.slot], ACT.Copy).then_inc(c_high_done, 1)

            def exp(b, u):
                if not b.exists:
                    return
                if b.i is None and b.c == 0 and u == 0:
                    queries_stored(act, 0)
                need(act, sc_mm, b.times(12, u + 1))
                need(act, pv_mm, b.times(4, -4 + u // CH + 1))
                act.activation(probs[:, u // CH, u % CH], ps_sc[:, u % 2, 0:HQ * NQ], ACT.Exp,
                               scale=SCALE).then_inc(exp_done, 1)

            def key_copy(b, m):
                if b.exists:
                    need(act, k_mm, b.times(2, m + 1))
                    need(act, kr_done, b.times(1, 0))
                    act.activation(k_f32[:, m, :], ps_w[:, 0:KVE], ACT.Identity, bias=bk_sb[:, m:m + 1])\
                        .then_inc(k_evac, 1)

            def key_first(b):
                if b.exists:
                    need(act, k_evac, b.times(2, 2))
                    need(act, k_stored, b.times(16))
                    act.activation(k_parts[:, 0, :, 0:KVE], k_f32[:], ACT.Copy).then_inc(k1_done, 1)

            def value_evac(b, c, chunks):
                if b.exists:
                    n = CHROWS[c + chunks - 1]
                    need(act, v_mm, b.times(3, c + chunks))
                    need(act, pv_mm, b.times(4, -4))
                    if c + chunks == CH:
                        need(act, xt_mm, b.times(1, -2))
                    act.activation(v_ones[0:n, b.slot, c:c + chunks, :, 0:D],
                                   ps_w[0:n, 0:chunks * C].rearrange("p (c h d) -> p c h d", c=chunks, h=H), ACT.Copy)\
                        .then_inc(v_evac, 1)

            def max_copy(b, h):
                if b.exists:
                    need(act, max_tr, b.times(2, h + 1))
                    need(act, max_loaded[h], b.times(16))
                    act.activation(max_rows[:, h, :], ps_max_t, ACT.Copy).then_inc(max_copied, 1)

            def high_part(loaded, slot, dst):
                act.wait_ge(raw_loaded[slot], loaded)
                act.activation(dst, w_raw[:, slot], ACT.Copy).then_inc(wh_done, 1)

            def gate_hidden(n):
                m = n % 2
                act.wait_ge(g_mm, n + 1)
                need(act, g_part, n - 1)
                act.activation(g_relu[:, m, :], banks[:, GATE_BANKS[n], 0:GW], ACT.Relu, bias=gb1_sb[:, m:m + 1])\
                    .then_inc(g_relu_done, 1)

            def first_step():
                value_evac(Batch(1), 0, 2)
                max_copy(Batch(0), 0)
                value_evac(Batch(1), 2, 1)
                context_high(Batch(3))
                key_copy(Batch(2), 0)
                exp(Batch(0), 0)
                key_copy(Batch(2), 1)
                exp(Batch(0), 1)

            def second_step():
                b = Batch(0)
                exp(b, 2)
                max_copy(b, 1)
                key_first(Batch(2))
                for u in range(3, 7):
                    exp(b, u)
                key_copy(Batch(3), 0)
                exp(b, 7)
                exp(b, 8)
                key_copy(Batch(3), 1)
                exp(b, 9)
                max_copy(Batch(1), 0)
                exp(b, 10)
                key_first(Batch(3))
                exp(b, 11)

            def output_evac(b):
                need(act, pv_mm, b.times(4, 4))
                need(act, o_tr, b.times(1))
                act.activation(o_full[:], ps_o[:, 0:4 * NQ], ACT.Copy).then_inc(o_copied, 1)

            def tokens_high(b):
                need(act, xt_mm, b.times(1, 1))
                at = b.times(NQ)
                dst = xt_parts[:, 0, :, at:at + NQ] if b.i is None else xt_parts[:, 0, :, bass.ds(at, NQ)]
                act.activation(dst, ps_xt.rearrange("p (a t) -> p a t", a=2), ACT.Copy).then_inc(xt_high_done, 1)

            def output_high(b):
                need(act, ot_mm, b.times(1, 1))
                act.activation(ot_high[:], ps_w[:, 0:2 * NQ].rearrange("p (a t) -> p a t", a=2), ACT.Copy)\
                    .then_inc(ot_high_done, 1)

            def last_steps(s):
                if s.c == B:
                    last = Batch(B - 1)
                    output_evac(last)
                    high_part(16, 0, w1_parts[:, 0, 0])
                    tokens_high(last + -1)
                    gate_hidden(0)
                    output_high(last)
                    gate_hidden(1)
                    high_part(16, 1, w1_parts[:, 1, 0])
                else:
                    gate_hidden(2)
                    gate_hidden(3)
                    tokens_high(Batch(B - 1))
                    gate_hidden(4)
                    gate_hidden(5)

            def step(s):
                if s.i is None and s.c <= 0:
                    return second_step() if s.exists else first_step()
                if s.i is None and s.c >= B:
                    return last_steps(s)
                old, last, nxt, new = s + -2, s + -1, s + 1, s + 3
                exp(s, 0)
                max_copy(s, 1)
                if last.exists:
                    output_evac(last)
                if nxt.exists_from(2):
                    value_evac(nxt, 0, 2)
                exp(s, 1)
                exp(s, 2)
                if nxt.exists_from(2):
                    value_evac(nxt, 2, 1)
                if old.exists:
                    tokens_high(old)
                exp(s, 3)
                exp(s, 4)
                exp(s, 5)
                if new.exists_from(EARLY):
                    context_high(new)
                if last.exists:
                    output_high(last)
                exp(s, 6)
                max_copy(nxt, 0)
                exp(s, 7)
                exp(s, 8)
                key_copy(new, 0)
                exp(s, 9)
                exp(s, 10)
                exp(s, 11)
                key_copy(new, 1)
                key_first(new)

            act.wait_ge(pad_set, 1)
            weight_high(WQ)
            context_high(Batch(0))
            weight_high(WK)
            context_high(Batch(1))
            weight_high(WV)
            query_high(0)
            act.wait_ge(small_loaded, 16)
            for m in range(2):
                key_copy(Batch(0), m)
                if m == 1:
                    key_first(Batch(0))
                query_evac(0, m)
            query_high(1)
            query_high(2)
            value_evac(Batch(0), 0, 2)
            value_evac(Batch(0), 2, 1)
            for g in range(1, NG):
                for m in range(2):
                    query_evac(g, m)
                if g == 1:
                    query_high(3)
                    for n in (WO, GW1):
                        weight_high(n)
                if g == 2:
                    context_high(Batch(2))
            for m in range(2):
                key_copy(Batch(1), m)
            key_first(Batch(1))
            steps(act, step)

            gate_hidden(6)
            gate_hidden(7)
            act.wait_ge(g_gate_mm, 1)
            act.wait_ge(late_loaded, 16 * 2)
            for start, n in ((0, NQ), (NQ, P - NQ)):
                act.activation(gate_t[:, start:start + n], banks[0:E, 7, 0:n], ACT.Identity, bias=gb2_sb[:, 0:1],
                               scale=1.0 / B).then_inc(g_t_done, 1)
            for n, (start, end) in enumerate(ROW_PARTS):
                act.wait_ge(g_exp_mm, n + 1)
                act.activation(row_part(0, n), banks[:, ROW_BANKS[n], 0:end - start], ACT.Copy).then_inc(g_row_done, 1)

            with act.Fori(1, E) as e:
                for s in range(2):
                    act.wait_ge(z1_mm, e * (2 * TT) + (s - 1) * TT)
                    high_part(e * 16 + 16, s, w1_parts[:, s, 0])
            def second_high(pair, c):
                if pair == 0 and c >= 2:
                    act.wait_ge(z1_mm, TT * (L1N - 3 + c))
                high_part(16 * (E + 2 * pair + c // 2 + 1), c % 2, w2_parts[:, pair, c, 0])

            for c in range(L2C - 1):
                second_high(0, c)
            for t in range(TT):
                act.wait_ge(h_tr, t + 1)
                act.activation(h_high[:, t], banks[:, 2 + 2 * (t % 2):4 + 2 * (t % 2), :], ACT.Relu)\
                    .then_inc(h_high_done, 1)
                if t == 1:
                    second_high(0, L2C - 1)
                if t % 2 == 1 and 1 < t < 2 * L2C + 2:
                    second_high(1, t // 2 - 1)
            with act.Fori(2, L2P) as ep:
                act.wait_ge(z2_mm, ep * TT - TT)
                for c in range(L2C):
                    high_part(ep * 32 + 16 * (E + c // 2 + 1), c % 2,
                              w2_parts[:, bass.ds(ep % 2, 1), c, 0].rearrange("p s a n -> p (s a) n"))

        @block.vector
        def _(dve):
            def halve_bits(start, end, aggregated, count):
                value, of = aggregated
                n = slice(start, end)
                dve.wait_ge(of, value)
                dve.tensor_scalar(half_var[:, n], mean_var[:, n, 1], EPS, 0.5, ALU.add, ALU.mult)\
                    .then_inc(eps_added, 1)
                dve.wait_ge(eps_added, count)
                dve.tensor_scalar(half_bits[:, n], half_var[:, n].bitcast(I32), 1, None,
                                  ALU.logical_shift_right).then_inc(bits_halved, 1)

            def query_stats(groups):
                for g in groups:
                    dve.wait_ge(x_loaded[g], 16)
                    for b in range(GB * g, GB * g + GB):
                        dve.bn_stats(q_stats[:, b, :], x_all[:, b, :]).then_inc(q_stat, 1)
                for b in range(GB * groups[0], GB * groups[-1] + GB):
                    dve.wait_ge(q_stat, b + 1)
                    dve.bn_aggr(mean_var[:, b, :], q_stats[:, b, :]).then_inc(q_aggr, 1)
                halve_bits(GB * groups[0], GB * groups[-1] + GB, (GB * groups[-1] + GB, q_aggr), groups[0] + 1)

            def query_norm(g):
                dve.wait_ge(root_done, ROOT_OPS * min(g + 1, ROOTS))
                need(dve, q_tr, g - 1)
                for j in range(GB):
                    b = GB * g + j
                    dve.tensor_scalar(xq[:, g % 2, j, :], x_all[:, b, :], mean_var[:, b, 0:1],
                                      rstd[:, b:b + 1], ALU.subtract, ALU.mult).then_inc(q_norm, 1)

            def query_low(g):
                dve.wait_ge(q_xhigh, g + 1)
                need(dve, q_mm, 2 * (g - 1))
                dve.tensor_tensor(xqt_low[:, g % 2], ps_qt[g % 2][:, :, 0:GW], xqt_high[:, g % 2], ALU.subtract)\
                    .then_inc(q_xlow, 1)

            def query_parts(g):
                dve.wait_ge(qr_done, g + 1)
                dve.tensor_copy(q_parts[g][:, 1], q_rest[:]).then_inc(q2_done, 1)
                dve.wait_ge(q2_done, g + 1)
                dve.tensor_tensor(q_parts[g][:, 2], q_rest[:], q_parts[g][:, 1], ALU.subtract)\
                    .then_inc(q3_done, 1)

            def weight_low(n):
                dve.wait_ge(w_high_done, n + 1)
                dve.tensor_tensor(w_low[:, n], w_f32[:, n], w_high[:, n], ALU.subtract).then_inc(w_low_done[n], 1)

            def key_second(b):
                need(dve, kr_done, b.times(1, 1))
                dve.tensor_copy(k_parts[:, 1, :, 0:KVE], k_rest[:]).then_inc(k2_done, 1)

            def reduce_max(b, k):
                if b.exists:
                    need(dve, max_mm, b.times(8, k + 1))
                    dve.tensor_reduce(maxima[:, b.slot, 2 * k:2 * k + 2], ps_max[k % 2][0:NQ, :, 0:NKV], AX_X, ALU.max)\
                        .then_inc(max_red, 1)

            def max_first(b, h):
                if b.exists:
                    need(dve, max_red, b.times(8, 4 * h + 4))
                    need(dve, max_tr, b.times(2, h - 1))
                    dve.tensor_copy(max_parts[:, h, 0, :], maxima[:, b.slot, HH * h:HH * h + HH]).then_inc(m1_done, 1)

            def max_second(b, h):
                if b.exists:
                    need(dve, m1_done, b.times(2, h + 1))
                    dve.tensor_tensor(max_parts[:, h, 1, :], maxima[:, b.slot, HH * h:HH * h + HH],
                                      max_parts[:, h, 0, :], ALU.subtract).then_inc(m2_done, 1)

            def gate_sum(n):
                g, m = n // 2, n % 2
                dve.wait_ge(g_relu_done, n + 1)
                dve.tensor_reduce(h_sums[:, m, g, :], g_relu[:, m, :].rearrange("p (b t) -> p t b", b=GB),
                                  AX_X, ALU.add).then_inc(g_part, 1)

            def step(s):
                old, last, nxt, new = s + -2, s + -1, s + 1, s + 2
                max_first(s, 1)
                max_second(s, 1)
                if s.i is None and s.c == 0:
                    query_parts(NG - 1)
                if old.exists:
                    need(dve, root_done, old.times(ROOT_OPS, ROOT_OPS) + ROOT_OPS * ROOTS)
                    dve.tensor_scalar(x_norm[:], x_mid[:, old.slot, :], mean_var[:, 0, 0:1], rstd[:, 0:1],
                                      ALU.subtract, ALU.mult).then_inc(xn_done, 1)
                if nxt.exists_from(1):
                    reduce_max(nxt, 0)
                    reduce_max(nxt, 1)
                if new.exists_from(2):
                    key_second(new)
                if last.exists:
                    need(dve, o_tr, last.times(1, 1))
                    sums = ps_o[0:NQ, :].rearrange("p (h w) -> p h w", w=VW)
                    dve.reciprocal(recip[:], sums[:, :, D]).then_inc(recip_done, 1)
                    need(dve, recip_done, last.times(1, 1))
                    dve.tensor_tensor(o_norm[:], sums[:, :, 0:D], recip[:].unsqueeze(2).to_broadcast([NQ, H, D]),
                                      ALU.mult).then_inc(o_normed, 1)
                if old.exists:
                    need(dve, xt_high_done, old.times(1, 1))
                    at = old.times(NQ)
                    cols = slice(at, at + NQ) if old.i is None else bass.ds(at, NQ)
                    dve.tensor_tensor(xt_parts[:, 1, :, cols], ps_xt.rearrange("p (a t) -> p a t", a=2),
                                      xt_parts[:, 0, :, cols], ALU.subtract).then_inc(xt_low_done, 1)
                if s.i is None and s.c == B + 1:
                    gate_sum(4)
                    gate_sum(5)
                reduce_max(nxt, 2)
                reduce_max(nxt, 3)
                max_first(nxt, 0)
                max_second(nxt, 0)
                if s.i is None and s.c == FIRST_STEP:
                    key_second(new)
                if last.exists:
                    need(dve, ot_high_done, last.times(1, 1))
                    dve.tensor_tensor(ot_low[:], ps_w[:, 0:2 * NQ].rearrange("p (a t) -> p a t", a=2), ot_high[:],
                                      ALU.subtract).then_inc(ot_low_done, 1)
                reduce_max(nxt, 4)
                if last.exists:
                    need(dve, out_mm, last.times(1, 1))
                    need(dve, xb_done, last.times(1, 1))
                    need(dve, xmid_stored[last.slot], last.uses(16) + -16)
                    dve.tensor_tensor(x_mid[:, last.slot, :], ps_w[0:NQ, 0:C], x_bias[:], ALU.add).then_inc(xmid_done, 1)
                if last.exists:
                    need(dve, xmid_done, last.times(1, 1))
                    need(dve, xn_done, last.times(1))
                    dve.bn_stats(stats[:], x_mid[:, last.slot, :]).then_inc(stat_done, 1)
                    need(dve, stat_done, last.times(1, 1))
                reduce_max(nxt, 5)
                if last.exists:
                    dve.bn_aggr(mean_var[:, 0, :], stats[:]).then_inc(aggr_done, 1)
                    halve_bits(0, 1, (last.times(1, 1), aggr_done), last.times(1, 1) + ROOTS)
                reduce_max(nxt, 6)
                reduce_max(nxt, 7)
                if s.i is None and s.c == B:
                    gate_sum(0)
                    gate_sum(1)
                    gate_sum(2)
                    gate_sum(3)

            dve.wait_ge(ones_set, 1)
            query_stats([0])
            weight_low(WQ)
            query_stats([1])
            query_norm(0)
            weight_low(WK)
            query_stats([2, 3])
            query_low(0)
            weight_low(WV)
            for g in range(1, NG):
                query_norm(g)
                if g == 2:
                    key_second(Batch(0))
            query_low(1)
            query_parts(0)
            query_low(2)
            query_low(3)
            query_parts(1)
            dve.wait_ge(small_loaded, 16)
            dve.wait_ge(late_loaded, 16 * 2)
            dve.tensor_copy(bv_wide[:], bv_sb.unsqueeze(2).to_broadcast([P, 2, NQ])).then_inc(bv_wide_done, 1)
            weight_low(WO)
            weight_low(GW1)
            query_parts(2)
            reduce_max(Batch(0), 0)
            dve.wait_ge(bias_mm, 1)
            dve.tensor_tensor(bias_row[:], ps_o[0:NQ, 0:C], bo_row[:], ALU.add).then_inc(bias_done, 1)
            reduce_max(Batch(0), 1)
            steps(dve, step)

            gate_sum(6)
            gate_sum(7)

            def add_first(e, s, t, base):
                dve.wait_ge(z1_mm, e * (2 * TT) + (s * TT + t + 1))
                gate_col = gates[:, t % PAT, C + e:C + e + 1] if isinstance(e, int) else \
                    gates[:, t % PAT, bass.ds(e + C, 1)]
                dve.scalar_tensor_tensor(out=acc[:, t, 512 * s:512 * s + 512], in0=banks[:, t % NB1, :],
                                         scalar=gate_col, in1=base[:, 512 * s:512 * s + 512],
                                         op0=ALU.mult, op1=ALU.add).then_inc(acc_done, 1)

            dve.wait_ge(g_row_done, 2)
            for s in range(2):
                for t in range(TT):
                    if 0 < t < PAT:
                        dve.wait_ge(rows_loaded[s][t], 32 if s == 0 else 16)
                    if (s, t) == (1, 0):
                        dve.wait_ge(g_row_done, 3)
                    add_first(0, s, t, b1_rows[:, t % PAT, :])
            with dve.Fori(1, E) as e:
                for s in range(2):
                    for t in range(TT):
                        add_first(e, s, t, acc[:, t, :])

            def add_second(ep, t):
                dve.wait_ge(z2_mm, ep * TT + (t + 1))
                for k in range(2):
                    gate_col = gates[:, t % PAT, C + 2 * ep + k:C + 2 * ep + k + 1] if isinstance(ep, int) else \
                        gates[:, t % PAT, bass.ds(ep * 2 + (C + k), 1)]
                    if k == 1:
                        dve.wait_ge(y_done, ep * (2 * TT) + (2 * t + 1))
                    dve.scalar_tensor_tensor(out=y[:, t, :], in0=banks[:, t % 2, C * k:C * k + C], scalar=gate_col,
                                             in1=y[:, t, :], op0=ALU.mult, op1=ALU.add).then_inc(y_done, 1)

            def hidden_low(t):
                dve.wait_ge(h_high_done, t + 1)
                ps = banks[:, 2 + 2 * (t % 2):4 + 2 * (t % 2), :].rearrange("p k n -> p (k n)")
                dve.scalar_tensor_tensor(out=h_low[:, t].rearrange("p k n -> p (k n)"), in0=ps, scalar=0.0,
                                         in1=h_high[:, t].rearrange("p k n -> p (k n)"),
                                         op0=ALU.max, op1=ALU.subtract).then_inc(h_low_done, 1)

            dve.wait_ge(y_ready, TT // PAT)
            hidden_low(0)
            for t in range(TT):
                if t + 1 < TT:
                    hidden_low(t + 1)
                add_second(0, t)
            with dve.Fori(1, L2P) as ep:
                for t in range(TT):
                    add_second(ep, t)

        @block.tensor
        def _(pe):
            pe.wait_ge(ident_set, 3)
            xqt, w_part = (xqt_high, xqt_low), (w_high, w_low)

            def query_transpose(g):
                pe.wait_ge(q_norm, GB * (g + 1))
                need(pe, q_xlow, g - 1)
                for j in range(GB):
                    for k in range(IT):
                        last = pe.transpose(ps_qt[g % 2][:, k, j * NQ:(j + 1) * NQ], xq[:, g % 2, j, P * k:P * k + P],
                                            ident[0:NQ, 0:NQ])
                last.then_inc(q_tr, 1)

            def query_project(g, m):
                pe.wait_ge(q_xlow, g + 1)
                need(pe, q_evac, 2 * g + m - 1)
                three(pe, ps_q[:, m, 0:GW], lambda a, k: w_part[a][:, WQ, k, P * m:P * m + P],
                      lambda a, k: xqt[a][:, g % 2, k, :], IT).then_inc(q_mm, 1)

            c_part = (c_high, c_low)

            def key_project(b, m):
                if not b.exists:
                    return
                if m == 0:
                    need(pe, c_low_done, b.times(1, 1))
                    need(pe, xmid_done, b.times(1, -3))
                    if b.i is None and b.c < 4:
                        need(pe, v_evac, 2 * min(b.c, 2))
                        need(pe, k_evac, 2 * b.c)
                else:
                    need(pe, k_evac, b.times(2, 1))
                three(pe, ps_w[:, 0:KVE], lambda a, k: w_part[a][:, WK, k, P * m:P * m + P],
                      lambda a, k: c_part[a][:, b.slot, k, :], IT).then_inc(k_mm, 1)

            def value_project(b, c):
                if not b.exists:
                    return
                n = CHROWS[c]
                if c == 0:
                    need(pe, k_evac, b.times(2, 2 if b.i is None and b.c < 2 else 4))
                    if b.i is None:
                        need(pe, xmid_done, b.times(1, -2))
                elif c == 2:
                    need(pe, v_evac, b.times(2, 1))
                three(pe, ps_w[0:n, (c % 2) * C:(c % 2 + 1) * C], lambda a, k: c_part[a][:, b.slot, k, P * c:P * c + n],
                      lambda a, k: w_part[a][:, WV, k, :], IT).then_inc(v_mm, 1)

            def max_scores(b, k):
                if not b.exists:
                    return
                if k % 4 == 0:
                    need(pe, stack_loaded[b.slot][k // 4], b.uses(96))
                need(pe, max_red, b.times(8, k - 1))
                if k == 1:
                    need(pe, max_copied, b.times(2))
                if k == 5:
                    need(pe, max_copied, b.times(2, 1))
                for n in range(2):
                    h = 2 * k + n
                    last = pe.matmul(ps_max[k % 2][0:NQ, n, 0:NKV], q_stack[0:QROWS, b.slot, h * NQ:(h + 1) * NQ],
                                     k_stack[0:QROWS, b.slot, h, 0:NKV], start=True, stop=True)
                last.then_inc(max_mm, 1)

            def max_transpose(b, h):
                if not b.exists:
                    return
                need(pe, m2_done, b.times(2, h + 1))
                need(pe, max_red, b.times(8, 8 if h else 4))
                pe.transpose(ps_max_t, max_parts[:, h].rearrange("p a h -> p (a h)"), ident_b[0:NQ, 0:NQ])\
                    .then_inc(max_tr, 1)

            def scores(b, u):
                if not b.exists:
                    return
                quarter, c = u // CH, u % CH
                if u % (2 * CH) == 0:
                    need(pe, max_loaded[u // (2 * CH)], b.times(16, 16))
                need(pe, exp_done, b.times(12, u - 1))
                for n in range(HQ):
                    head = HQ * quarter + n
                    last = pe.matmul(ps_sc[:, u % 2, n * NQ:(n + 1) * NQ],
                                     k_stack[0:SROWS, b.slot, head, P * c:P * c + P],
                                     q_stack[0:SROWS, b.slot, head * NQ:(head + 1) * NQ], start=True, stop=True)
                last.then_inc(sc_mm, 1)

            def weigh_values(b, quarter):
                if not b.exists:
                    return
                need(pe, exp_done, b.times(12, CH * (quarter + 1)))
                if quarter == 0:
                    need(pe, v_evac, b.times(2, 2))
                    need(pe, o_normed, b.times(1))
                    if b.i is None and b.c == 0:
                        pe.wait_ge(bias_done, 1)
                for c in range(CH):
                    n = CHROWS[c]
                    for g in range(HQ):
                        last = pe.matmul(ps_o[VW * g:VW * g + VW, quarter * NQ:(quarter + 1) * NQ],
                                         v_ones[0:n, b.slot, c, HQ * quarter + g, :],
                                         probs[0:n, quarter, c, g * NQ:(g + 1) * NQ],
                                         start=(c == 0), stop=(c == CH - 1))
                last.then_inc(pv_mm, 1)

            def output_transpose(b):
                if not b.exists:
                    return
                need(pe, o_copied, b.times(1, 1))
                for hb in range(4):
                    last = pe.transpose(ps_o[0:NQ, P * hb:P * hb + P], o_full[:, hb * NQ:(hb + 1) * NQ], ident[:])
                last.then_inc(o_tr, 1)

            def output_back(b):
                if not b.exists:
                    return
                need(pe, o_normed, b.times(1, 1))
                need(pe, v_evac, b.times(2, 6))
                need(pe, xt_low_done, b.times(1))
                for k in range(IT):
                    last = pe.transpose(ps_w[:, k * NQ:(k + 1) * NQ],
                                        o_norm[:, HH * k:HH * k + HH, :].rearrange("p h d -> p (h d)"),
                                        ident[0:NQ, 0:NQ])
                last.then_inc(ot_mm, 1)

            def output_project(b):
                if not b.exists:
                    return
                need(pe, ot_low_done, b.times(1, 1))
                ot = (ot_high, ot_low)
                three(pe, ps_w[0:NQ, 0:C], lambda a, k: ot[a][:, k, :], lambda a, k: w_part[a][:, WO, k, :], IT)\
                    .then_inc(out_mm, 1)

            def token_transpose(b):
                if not b.exists:
                    return
                need(pe, xn_done, b.times(1, 1))
                for k in range(IT):
                    last = pe.transpose(ps_xt[:, k * NQ:(k + 1) * NQ], x_norm[:, P * k:P * k + P], ident[0:NQ, 0:NQ])
                last.then_inc(xt_mm, 1)

            def gate_hidden(n):
                g, m = n // 2, n % 2
                pe.wait_ge(xt_low_done, GB * (g + 1))
                if n in (4, 5):
                    pe.wait_ge(g_relu_done, n - 3)
                elif n > 5:
                    pe.wait_ge(exp_done, 12 * B)
                three(pe, banks[:, GATE_BANKS[n], 0:GW], lambda a, k: w_part[a][:, GW1, k, P * m:P * m + P],
                      lambda a, k: xt_parts[:, a, k, GW * g:GW * g + GW], IT).then_inc(g_mm, 1)

            def first_step():
                max_scores(Batch(0), 2)
                max_scores(Batch(0), 3)
                value_project(Batch(1), 0)
                value_project(Batch(1), 1)
                max_transpose(Batch(0), 0)
                max_scores(Batch(0), 4)
                value_project(Batch(1), 2)
                max_scores(Batch(0), 5)
                key_project(Batch(2), 0)
                scores(Batch(0), 0)
                max_scores(Batch(0), 6)
                key_project(Batch(2), 1)
                max_scores(Batch(0), 7)
                scores(Batch(0), 1)

            def second_step():
                b, nxt = Batch(0), Batch(1)
                key_project(Batch(3), 0)
                scores(b, 2)
                max_transpose(b, 1)
                scores(b, 3)
                scores(b, 4)
                scores(b, 5)
                weigh_values(b, 0)
                max_scores(nxt, 0)
                max_scores(nxt, 1)
                scores(b, 6)
                max_scores(nxt, 2)
                weigh_values(b, 1)
                scores(b, 7)
                max_scores(nxt, 3)
                key_project(Batch(3), 1)
                scores(b, 8)
                max_transpose(nxt, 0)
                scores(b, 9)
                max_scores(nxt, 4)
                weigh_values(b, 2)
                scores(b, 10)
                max_scores(nxt, 5)
                max_scores(nxt, 6)
                scores(b, 11)
                max_scores(nxt, 7)

            def first_layer(e, s, t, first):
                if t == 0:
                    pe.wait_ge(wl_done, e * 2 + (s + 1))
                if not (first and s * TT + t < NB1):
                    pe.wait_ge(acc_done, e * (2 * TT) + (s * TT + t - NB1 + 1))
                three(pe, banks[:, t % NB1, :], lambda a, k: xt_parts[:, a, k, P * t:P * t + P],
                      lambda a, k: w1_parts[:, s, a, k, :], IT).then_inc(z1_mm, 1)

            def last_steps(s):
                if s.c == B:
                    last = Batch(B - 1)
                    weigh_values(last, 3)
                    output_transpose(last)
                    token_transpose(last + -1)
                    gate_hidden(0)
                    output_back(last)
                    gate_hidden(1)
                    output_project(last)
                else:
                    for n in range(2, 5):
                        gate_hidden(n)
                    token_transpose(Batch(B - 1))
                    gate_hidden(5)

            def step(s):
                if s.i is None and s.c <= 0:
                    return second_step() if s.exists else first_step()
                if s.i is None and s.c >= B:
                    return last_steps(s)
                old, last, nxt, new = s + -2, s + -1, s + 1, s + 3
                scores(s, 0)
                weigh_values(last, 3)
                max_transpose(s, 1)
                early = s.i is None and s.c == 1
                if not early:
                    max_scores(nxt, 0)
                value_project(nxt, 0)
                value_project(nxt, 1)
                if early:
                    max_scores(nxt, 0)
                scores(s, 1)
                if nxt.exists_from(1):
                    max_scores(nxt, 1)
                scores(s, 2)
                output_transpose(last)
                if nxt.exists_from(2):
                    value_project(nxt, 2)
                token_transpose(old)
                scores(s, 3)
                max_scores(nxt, 2)
                scores(s, 4)
                max_scores(nxt, 3)
                scores(s, 5)
                weigh_values(s, 0)
                max_scores(nxt, 4)
                output_back(last)
                scores(s, 6)
                weigh_values(s, 1)
                max_transpose(nxt, 0)
                scores(s, 7)
                output_project(last)
                max_scores(nxt, 5)
                scores(s, 8)
                max_scores(nxt, 6)
                key_project(new, 0)
                scores(s, 9)
                weigh_values(s, 2)
                scores(s, 10)
                max_scores(nxt, 7)
                scores(s, 11)
                key_project(new, 1)

            query_transpose(0)
            pe.wait_ge(w_low_done[WK], 1)
            for m in range(2):
                key_project(Batch(0), m)
                if m == 0:
                    pe.wait_ge(w_low_done[WQ], 1)
                query_project(0, m)
            query_transpose(1)
            query_transpose(2)
            pe.wait_ge(w_low_done[WV], 1)
            pe.wait_ge(ones_set, 2)
            for c in range(CH):
                value_project(Batch(0), c)
            for g in range(1, NG):
                for m in range(2):
                    query_project(g, m)
                if g == 1:
                    query_transpose(3)
            for m in range(2):
                key_project(Batch(1), m)
                max_scores(Batch(0), m)
                if m == 0:
                    pe.wait_ge(bv_wide_done, 1)
                    for k in range(IT):
                        last = pe.matmul(ps_o[0:NQ, 0:C], bv_wide[:, k, :], w_f32[:, WO, k, :],
                                         start=(k == 0), stop=(k == 1))
                    last.then_inc(bias_mm, 1)
            pe.wait_ge(stack_set, 16)
            pe.wait_ge(q_evac, 2 * NG)
            for n in (WO, GW1):
                pe.wait_ge(w_low_done[n], 1)
            steps(pe, step)

            gate_hidden(6)
            gate_hidden(7)
            for n in range(2 * NG):
                if n == 2 * NG - 2:
                    first_layer(0, 0, 0, True)
                pe.wait_ge(g_part, n + 1)
                last = pe.matmul(banks[0:E, 7, 0:NQ], gw2_sb[:, n % 2, :], h_sums[:, n % 2, n // 2, :],
                                 start=(n == 0), stop=(n == 2 * NG - 1))
            last.then_inc(g_gate_mm, 1)
            first_layer(0, 0, 1, True)
            pe.wait_ge(g_t_done, 2)
            pe.wait_ge(eb_loaded, 32)
            for n, (start, end) in enumerate(ROW_PARTS):
                need(pe, g_row_done, n - 1)
                pe.matmul(banks[:, ROW_BANKS[n], 0:end - start], gate_t[:], eb_sb[:, start:end], start=True, stop=True)\
                    .then_inc(g_exp_mm, 1)
            for t in range(2, 6):
                first_layer(0, 0, t, True)
            pe.wait_ge(g_row_done, 2)
            for s in range(2):
                for t in range(TT):
                    if s * TT + t >= 6:
                        first_layer(0, s, t, True)
            with pe.Fori(1, E) as e:
                for s in range(2):
                    for t in range(TT):
                        first_layer(e, s, t, False)

            def hidden_transpose(t):
                pe.wait_ge(acc_done, 2 * TT * (E - 1) + TT + t + 1)
                if t < 2:
                    pe.wait_ge(acc_done, 2 * TT * E - NB1 + 2 * (t % 2) + 4)
                else:
                    pe.wait_ge(h_low_done, t - 1)
                for k in range(OT):
                    last = pe.transpose(banks[:, 2 + 2 * (t % 2) + k // 4, P * (k % 4):P * (k % 4) + P],
                                        acc[:, t, P * k:P * k + P], ident[:])
                last.then_inc(h_tr, 1)

            h_part = (h_high, h_low)

            def second_layer(ep, slot, t, first):
                if first:
                    pe.wait_ge(h_low_done, t + 1)
                if not (first and t < 2):
                    pe.wait_ge(y_done, ep * (2 * TT) + 2 * (t - 1))
                n = 0
                for c in range(L2C):
                    if t == 0:
                        pe.wait_ge(wl_done, ep * L2C + (L1N + c + 1))
                    for a, b in ((0, 0), (0, 1), (1, 0)):
                        for k in range(2):
                            w = w2_parts[:, slot, c, b, k, :]
                            last = pe.matmul(banks[:, t % 2, :], h_part[a][:, t, 2 * c + k, :], w,
                                             start=(n == 0), stop=(n == 3 * OT - 1))
                            n += 1
                last.then_inc(z2_mm, 1)

            hidden_transpose(0)
            for t in range(TT):
                if t + 1 < TT:
                    hidden_transpose(t + 1)
                second_layer(0, 0, t, True)
            with pe.Fori(1, L2P) as ep:
                for t in range(TT):
                    second_layer(ep, bass.ds(ep % 2, 1), t, False)


def kernel(x, ctx_1024, L0_xattn_w_q, L0_xattn_b_q, L0_xattn_w_kv, L0_xattn_b_kv, L0_xattn_w_out, L0_xattn_b_out,
           L0_ffn_gW1, L0_ffn_gb1, L0_ffn_gW2, L0_ffn_gb2, L0_ffn_eW1, L0_ffn_eb1, L0_ffn_eW2, L0_ffn_eb2):
    import numpy as np
    import concourse.bacc as bacc
    from concourse.bass_utils import run_bass_kernel_spmd

    def a(v):
        return np.asarray(v)

    order = np.array([(2 * (p % HH) + m) * D + p // HH for m in range(2) for p in range(P)])
    w_kv, b_kv = a(L0_xattn_w_kv), a(L0_xattn_b_kv)

    def tiles(w):
        return w.reshape(IT, P, -1).transpose(1, 0, 2)

    def halves(v):
        return v.reshape(2, P).T

    e1, e2 = a(L0_ffn_eW1), a(L0_ffn_eW2)
    arrays = {
        "x": a(x),
        "ctx_t": a(ctx_1024).transpose(2, 0, 1).reshape(IT, P, B, NKV).transpose(1, 2, 0, 3),
        "wq": tiles(a(L0_xattn_w_q)[:, order]), "wk": tiles(w_kv[:, :C][:, order]),
        "wv": tiles(w_kv[:, C:]), "wo": tiles(a(L0_xattn_w_out)), "bo": a(L0_xattn_b_out).reshape(1, C),
        "gw1": tiles(a(L0_ffn_gW1).T), "gb2": a(L0_ffn_gb2).reshape(E, 1),
        "small": np.concatenate([halves(a(L0_xattn_b_q)[order]), halves(b_kv[:C][order]), halves(b_kv[C:]),
                                 halves(a(L0_ffn_gb1)), a(L0_ffn_gW2).reshape(E, 2, P).transpose(2, 1, 0)
                                 .reshape(P, 2 * E)], axis=1),
        "w1": e1.reshape(E, 2, 512, IT, P).transpose(0, 1, 4, 3, 2).reshape(2 * E, P, IT, 512),
        "eb": np.concatenate([a(L0_ffn_eb1), a(L0_ffn_eb2)], axis=1),
        "w2": e2.reshape(E // 2, 2, C, OT // 2, 2, P).transpose(0, 3, 5, 4, 1, 2).reshape(2 * E, P, 2, 512),
    }
    arrays = {k: np.ascontiguousarray(v) for k, v in arrays.items()}
    nc = bacc.Bacc("TRN2", target_bir_lowering=False, num_devices=1)
    args = {k: nc.dram_tensor(f"in_{k}", v.shape, mybir.dt.from_np(v.dtype), kind="ExternalInput").ap()
            for k, v in arrays.items()}
    out = nc.dram_tensor("out", (T, C), F32, kind="ExternalOutput").ap()
    build(nc, out=out, **args)
    r = run_bass_kernel_spmd(nc, [{f"in_{k}": v for k, v in arrays.items()}], core_ids=[0])
    return r.results[0]["out"].reshape(B, NQ, C)
```
